# Optimizing a Trainium2 kernel written in Bass

```python
import numpy as np
import jax
import jax.numpy as jnp

def _softmax(x, axis=-1):
    return jax.nn.softmax(x, axis=axis)

def _gelu(x):
    return jax.nn.gelu(x, approximate=True)

def _silu(x):
    return jax.nn.silu(x)

def _sigmoid(x):
    return jax.nn.sigmoid(x)

def _layernorm(x, axis=-1, eps=1e-05):
    m = jnp.mean(x, axis=axis, keepdims=True)
    v = jnp.var(x, axis=axis, keepdims=True)
    return (x - m) / jnp.sqrt(v + eps)

def _scatter_add(tgt, idx, src, axis=0):
    return tgt.at[idx].add(src)

def _segment_sum(src, seg, n):
    return jax.ops.segment_sum(src, seg, n)
kernel_name = 'mk_pixart_resid_d1_seqx_r4_a1d9ce'

def setup_inputs(seed: int=0):
    np.random.seed(seed)
    _w = jnp.asarray

    def _rec_inputs():
        import jax
        import jax.numpy as jnp
        _rk = jax.random.key(seed)
        x = 2.818e-05 + 1 * jax.random.normal(jax.random.fold_in(_rk, 1), (8, 256, 256), jnp.float32)
        _lenS = 256 - jax.random.randint(jax.random.fold_in(_rk, 7), (8,), 0, max(1, 256 // 4) + 1, jnp.int32)
        _lenS2 = 77 - jax.random.randint(jax.random.fold_in(_rk, 8), (8,), 0, max(1, 77 // 4) + 1, jnp.int32)
        _ctx_1024P = jax.random.normal(jax.random.fold_in(_rk, 11), (8, 16, 256), jnp.float32)
        _ctx_1024c = jax.random.dirichlet(jax.random.fold_in(_rk, 511), 0.3 * jnp.ones((16,), jnp.float32), (8, 77))
        _ctx_1024t = jnp.einsum('bsk,bkd->bsd', _ctx_1024c, _ctx_1024P)
        _ctx_1024t = _ctx_1024t * jax.lax.rsqrt(jnp.mean(jnp.square(_ctx_1024t)) + 1e-12) * 0.953939
        ctx_1024 = -0.000391444 + 0.999954 * (_ctx_1024t + 0.3 * jax.random.normal(jax.random.fold_in(_rk, 611), (8, 77, 256), jnp.float32))
        condB_pt = jax.random.uniform(jax.random.fold_in(_rk, 13), (8,), jnp.float32, 0.0, 226.919)
        return (x, ctx_1024, condB_pt, _lenS2)
    x, ctx_1024, condB_pt, _lenS2 = _rec_inputs()

    def _L0_xcond_setup():
        import jax, jax.numpy as jnp
        import numpy as np
        N, L, H, Q = (64, 258, 256, 64)
        WINDOW = 16.0
        DEV_POW = 128.0
        key = jax.random.key(seed)
        k1, k2, k3, k4, k5, k6 = jax.random.split(key, 6)
        encoder_outputs = jax.random.normal(k1, (N, L, H), dtype=jnp.float32)
        decoder_h_t = jax.random.normal(k2, (N, Q, H), dtype=jnp.float32)
        src_len = jax.random.randint(k3, (N,), 32, L + 1).astype(jnp.int32)
        p_t = jax.random.uniform(k4, (N,), dtype=jnp.float32) * (src_len.astype(jnp.float32) - 1.0)
        W_a = jax.random.normal(k5, (H, H), dtype=jnp.float32) * (1.0 / np.sqrt(H))
        W_c = jax.random.normal(k6, (H, 2 * H), dtype=jnp.float32) * (1.0 / np.sqrt(2 * H))
        return {'encoder_outputs': encoder_outputs, 'decoder_h_t': decoder_h_t, 'src_len': src_len, 'p_t': p_t, 'W_a': W_a, 'W_c': W_c}
    _L0_xcond_all = _L0_xcond_setup()
    _L0_xcond_in = {k: v for k, v in _L0_xcond_all.items() if k in ('W_a', 'W_c')}
    del _L0_xcond_all

    def _L0_ffn_setup():
        import jax, jax.numpy as jnp
        import numpy as np
        H = 16
        TOP_K = 2
        LN_EPS = 1e-05
        key = jax.random.key(seed)
        ks = jax.random.split(key, 8)
        B, S, E, NE = (2, 256, 256, 8)
        w = lambda k, shp: jax.random.normal(k, shp, dtype=jnp.float32) * 0.02
        return {'x': jax.random.normal(ks[0], (B, S, E), dtype=jnp.float32), 'rW1': w(ks[1], (E // 2, E)), 'rb1': jnp.zeros((E // 2,), jnp.float32), 'ln_g': jnp.ones((E // 2,), jnp.float32), 'ln_b': jnp.zeros((E // 2,), jnp.float32), 'rW2': w(ks[2], (NE, E // 2)), 'rb2': jnp.zeros((NE,), jnp.float32), 'qW': w(ks[3], (NE, E, E)), 'qb': jnp.zeros((NE, E), jnp.float32), 'kW': w(ks[4], (NE, E, E)), 'kb': jnp.zeros((NE, E), jnp.float32), 'vW': w(ks[5], (NE, E, E)), 'vb': jnp.zeros((NE, E), jnp.float32), 'oW': w(ks[6], (NE, E, E)), 'ob': jnp.zeros((NE, E), jnp.float32)}
    _L0_ffn_all = _L0_ffn_setup()
    _L0_ffn_in = {k: v for k, v in _L0_ffn_all.items() if k in ('rW1', 'rb1', 'ln_g', 'ln_b', 'rW2', 'rb2', 'qW', 'qb', 'kW', 'kb', 'vW', 'vb', 'oW', 'ob')}
    del _L0_ffn_all
    return {'x': x, 'ctx_1024': ctx_1024, 'condB_pt': condB_pt, '_lenS2': _lenS2, 'L0_xcond_W_a': _L0_xcond_in['W_a'], 'L0_xcond_W_c': _L0_xcond_in['W_c'], 'L0_ffn_rW1': _L0_ffn_in['rW1'], 'L0_ffn_rb1': _L0_ffn_in['rb1'], 'L0_ffn_ln_g': _L0_ffn_in['ln_g'], 'L0_ffn_ln_b': _L0_ffn_in['ln_b'], 'L0_ffn_rW2': _L0_ffn_in['rW2'], 'L0_ffn_rb2': _L0_ffn_in['rb2'], 'L0_ffn_qW': _L0_ffn_in['qW'], 'L0_ffn_qb': _L0_ffn_in['qb'], 'L0_ffn_kW': _L0_ffn_in['kW'], 'L0_ffn_kb': _L0_ffn_in['kb'], 'L0_ffn_vW': _L0_ffn_in['vW'], 'L0_ffn_vb': _L0_ffn_in['vb'], 'L0_ffn_oW': _L0_ffn_in['oW'], 'L0_ffn_ob': _L0_ffn_in['ob']}

def reference(x, ctx_1024, condB_pt, _lenS2, L0_xcond_W_a, L0_xcond_W_c, L0_ffn_rW1, L0_ffn_rb1, L0_ffn_ln_g, L0_ffn_ln_b, L0_ffn_rW2, L0_ffn_rb2, L0_ffn_qW, L0_ffn_qb, L0_ffn_kW, L0_ffn_kb, L0_ffn_vW, L0_ffn_vb, L0_ffn_oW, L0_ffn_ob):
    import jax
    import jax.numpy as jnp

    def _L0_xcond_ref(encoder_outputs, decoder_h_t, src_len, p_t, W_a, W_c):
        import jax, jax.numpy as jnp
        import numpy as np
        N, L, H, Q = (64, 258, 256, 64)
        WINDOW = 16.0
        DEV_POW = 128.0
        n, l, h = encoder_outputs.shape
        idx = jnp.arange(l, dtype=jnp.float32)
        src_end = src_len.astype(jnp.float32)
        attn_start = jnp.maximum(p_t - WINDOW, 0.0)
        attn_end = jnp.minimum(p_t + WINDOW, src_end)
        mask = (idx[None, :] < attn_start[:, None]) | (idx[None, :] > attn_end[:, None])
        score = jnp.einsum('nqh,hk,nlk->nql', decoder_h_t, W_a, encoder_outputs)
        score = jnp.where(mask[:, None, :], -1000000000.0, score)
        align = jax.nn.softmax(score, axis=2)
        gauss = jnp.exp(-(idx[None, :] - p_t[:, None]) ** 2 / DEV_POW)
        align = align * gauss[:, None, :]
        context = jnp.einsum('nql,nlh->nqh', align, encoder_outputs)
        cat = jnp.concatenate([context, decoder_h_t], axis=2)
        return jnp.tanh(cat @ W_c.T)

    def _L0_ffn_ref(x, rW1, rb1, ln_g, ln_b, rW2, rb2, qW, qb, kW, kb, vW, vb, oW, ob):
        import jax, jax.numpy as jnp
        import numpy as np
        H = 16
        TOP_K = 2
        LN_EPS = 1e-05
        B, S, E = x.shape
        NE = qW.shape[0]
        Dh = E // H
        scale = 1.0 / jnp.sqrt(jnp.asarray(Dh, x.dtype))
        h = x @ rW1.T + rb1
        mu = h.mean(-1, keepdims=True)
        var = ((h - mu) ** 2).mean(-1, keepdims=True)
        h = (h - mu) * jax.lax.rsqrt(var + LN_EPS) * ln_g + ln_b
        h = jax.nn.relu(h)
        logits = h @ rW2.T + rb2
        probs = jax.nn.softmax(logits, axis=-1)
        tp, ti = jax.lax.top_k(probs, TOP_K)
        tp = tp / tp.sum(-1, keepdims=True)
        expert_mask = (jax.nn.one_hot(ti, NE, dtype=probs.dtype) * tp[..., None]).sum(-2)
        gates = jnp.moveaxis(expert_mask, -1, 0)

        def expert_step(acc, params):
            qw, qb_, kw, kb_, vw, vb_, ow, ob_, g = params
            q = (x @ qw.T + qb_).reshape(B, S, H, Dh).transpose(0, 2, 1, 3)
            k = (x @ kw.T + kb_).reshape(B, S, H, Dh).transpose(0, 2, 1, 3)
            v = (x @ vw.T + vb_).reshape(B, S, H, Dh).transpose(0, 2, 1, 3)
            scores = jnp.einsum('bhqd,bhkd->bhqk', q, k) * scale
            p = jax.nn.softmax(scores, axis=-1)
            o = jnp.einsum('bhqk,bhkd->bhqd', p, v)
            o = o.transpose(0, 2, 1, 3).reshape(B, S, E) @ ow.T + ob_
            return (acc + o * g[..., None], None)
        out, _ = jax.lax.scan(expert_step, jnp.zeros_like(x), (qW, qb, kW, kb, vW, vb, oW, ob, gates))
        return out
    x = x + _L0_xcond_ref(ctx_1024, _layernorm(x, axis=-1), _lenS2, condB_pt, L0_xcond_W_a, L0_xcond_W_c)
    x = x + _L0_ffn_ref(_layernorm(x, axis=-1), L0_ffn_rW1, L0_ffn_rb1, L0_ffn_ln_g, L0_ffn_ln_b, L0_ffn_rW2, L0_ffn_rb2, L0_ffn_qW, L0_ffn_qb, L0_ffn_kW, L0_ffn_kb, L0_ffn_vW, L0_ffn_vb, L0_ffn_oW, L0_ffn_ob)
    return x

_drawn_inputs = setup_inputs


def setup_inputs(seed=0):
    import zlib

    import numpy as np

    out = dict(_drawn_inputs(seed))
    spreads = {'L0_ffn_rb1': (0.0, 0.273),
     'L0_ffn_ln_g': (1.0, 0.537),
     'L0_ffn_ln_b': (0.0, 0.409),
     'L0_ffn_rb2': (0.0, 0.1),
     'L0_ffn_qb': (0.0, 0.8),
     'L0_ffn_kb': (0.0, 0.8),
     'L0_ffn_vb': (0.0, 0.399),
     'L0_ffn_ob': (0.0, 0.1)}
    factors = {'L0_ffn_qW': 8.0, 'L0_ffn_kW': 8.0, 'L0_ffn_vW': 8.0, 'L0_ffn_oW': 2.705}
    for name, (base, spread) in spreads.items():
        noise = np.random.default_rng([zlib.crc32(name.encode()), seed]).standard_normal(out[name].shape)
        drawn = base * np.exp(spread * noise) if base else spread * noise
        out[name] = jnp.asarray(drawn.astype(out[name].dtype))
    for name, factor in factors.items():
        out[name] = (out[name] * factor).astype(out[name].dtype)
    return out
```

```python
from contextlib import ExitStack

import concourse.bass as bass
from concourse import mybir

ALU = mybir.AluOpType
ACT = mybir.ActivationFunctionType
AX = mybir.AxisListType
F32 = mybir.dt.float32
BF16 = mybir.dt.bfloat16
I32 = mybir.dt.int32


class Step:

    def __init__(self, eng, sem):
        self.eng, self.sem, self.done = eng, sem, 0

    def begin(self, turn, per):
        self.turn, self.per, self.local = turn, per, 0

    def __call__(self, ins, apart=None):
        self.local += 1
        ins.then_inc(self.sem, 1)
        self.eng.wait_ge(self.sem, self.turn * self.per + (self.done + self.local))
        if apart:
            apart(self.eng)

    def end(self, turns):
        assert self.local == self.per, self.local
        self.done += turns * self.per


def pixart_block(nc, x, ctx_e, ctx_t, p_t, src_len, waT, wcT, rw1T, rb1, ln_g, ln_b, rw2T, rb2,
                 qwT, qb, kwT, kb, vwT, vb, owT, ob, out):
    B, S, E = x.shape
    L = ctx_e.shape[1]
    NE = qwT.shape[0]
    R = rw1T.shape[1]
    H = 16
    D = E // H
    P = 128
    TT = S // P
    KT = E // P
    NT = B * TT
    G = 4
    NG = H // G
    V1 = D + 1
    KR = 6 * D
    KM = KR + 2
    SCALE = float(D) ** -0.5
    WINDOW, DEV_POW, NEG, EPS = 16.0, 128.0, 1e9, 1e-5
    assert TT == 2 and KT == 2 and NG == 4 and E == H * D and NE % 2 == 0 and R == P
    NJ = NE // 2
    SLOTS = [(0, 0), (1, 0), (0, 1), (1, 1), (0, 2), (2, 0)]

    with ExitStack() as st:
        def sb(name, shape, dt=F32):
            return st.enter_context(nc.sbuf_tensor(name, shape, dt))

        def psum(name):
            return st.enter_context(nc.psum_tensor(name, [P, 512], F32))

        def sem(name):
            return st.enter_context(nc.semaphore(name))

        acc = sb("acc", [P, NT, E])
        xT = sb("xT", [P, B, KT, S])
        gates = sb("gates", [P, NE * NT])
        ident = sb("ident", [P, P])
        ident_bf = sb("ident_bf", [P, P], BF16)
        enc = sb("enc", [L, E])
        encT = sb("encT", [P, KT, B * L])
        wa = sb("wa", [P, KT, E])
        wc = sb("wc", [P, 2 * KT, E])
        waenc = sb("waenc", [P, KT, B * L])
        pt = sb("pt", [P, B])
        len_i = sb("len_i", [P, B], I32)
        len_f = sb("len_f", [P, B])
        w_start = sb("w_start", [P, B])
        w_end = sb("w_end", [P, B])
        idx = sb("idx", [P, L])
        keep = sb("keep", [P, B, L])
        keep2 = sb("keep2", [P, B, L])
        fill = sb("fill", [P, B, L])
        gauss = sb("gauss", [P, B, L])
        rw1 = sb("rw1", [P, KT, R])
        rw2 = sb("rw2", [R, NE])
        rb1_b = sb("rb1_b", [P, R])
        lng_b = sb("lng_b", [P, R])
        lnb_b = sb("lnb_b", [P, R])
        rb2_b = sb("rb2_b", [P, NE])
        obr = sb("obr", [NE, E])
        mhalf = sb("mhalf", [P, TT])
        carry = sb("carry", [P, 16])
        stats = sb("stats", [P, TT, 6])
        mv = sb("mv", [P, TT, 2])
        veps = sb("veps", [P, TT])
        rstd = sb("rstd", [P, TT])
        hn = sb("hn", [P, TT, E])
        hnT = sb("hnT", [P, KT, S])
        sc = sb("sc", [P, TT, L])
        smx = sb("smx", [P, TT])
        ssum = sb("ssum", [P, TT])
        al = sb("al", [P, TT, L])
        alT = sb("alT", [L, S])
        cxT = sb("cxT", [P, KT, S])
        th = sb("th", [P, TT, E])
        rh = sb("rh", [P, TT, R])
        rhT = sb("rhT", [P, S])
        lg = sb("lg", [P, NT, NE])
        rank = sb("rank", [P, NE])
        pr = sb("pr", [P, NT, NE])
        pr2 = sb("pr2", [P, NT, NE])
        eq = sb("eq", [P, NT, NE])
        oh1 = sb("oh1", [P, NT, NE])
        oh2 = sb("oh2", [P, NT, NE])
        r1 = sb("r1", [P, NT])
        r2 = sb("r2", [P, NT])
        r3 = sb("r3", [P, NT])
        gt = sb("gt", [P, NT, NE])
        gT = sb("gT", [NE, NT, P])
        xs = [sb(f"xs{p}", [P, KT, S]) for p in range(2)]
        wqkv = [sb(f"wqkv{p}", [P, 3, KT, E]) for p in range(2)]
        bqkv = [sb(f"bqkv{p}", [P, 3, E]) for p in range(2)]
        wo = [sb(f"wo{p}", [P, KT, E]) for p in range(2)]
        q32 = sb("q32", [P, TT * H, D])
        k32 = sb("k32", [P, TT * H, D])
        rest = [sb(f"rest{n}", [P, TT * H, D]) for n in range(2)]
        qpack = sb("qpack", [P, TT * H, KR], BF16)
        kpack = sb("kpack", [P, TT * H, KM], BF16)
        Qp = [sb(f"Qp{p}", [KM, H, S], BF16) for p in range(2)]
        Kp = [sb(f"Kp{p}", [KM, H, S], BF16) for p in range(2)]
        vaug = [sb(f"vaug{p}", [P, TT, H, V1]) for p in range(2)]
        negm = [sb(f"negm{p}", [P, TT, G]) for p in range(2)]
        mhl = [sb(f"mhl{p}", [P, TT, 2 * G], BF16) for p in range(2)]
        mT = [sb(f"mT{p}", [2 * G, S], BF16) for p in range(2)]
        NP_ = 4
        pexp = [sb(f"pexp{n}", [P, TT, S]) for n in range(NP_)]
        oun = sb("oun", [P, NG, S])
        rcp = sb("rcp", [P, TT, H])
        rgt = sb("rgt", [P, TT, H])
        onm = sb("onm", [P, TT, H, D])
        onT = sb("onT", [P, KT, S])

        NS = 3
        S_BANK, BACK = (0, 1, 2, 1), (4, 2, 4, 2)
        psS = [psum(f"psS{n}") for n in range(NS)]
        psT = [psum(f"psT{n}") for n in range(2)]
        psV = psum("psV")
        psM = [psum("psA"), psum("psB")]

        x_in, const_in, bc_in, enc_in = sem("x_in"), sem("const_in"), sem("bc_in"), sem("enc_in")
        w_in, wo_in, mrow_in, stored = sem("w_in"), sem("wo_in"), sem("mrow_in"), sem("stored")
        xs_in = [sem(f"xs_in{p}") for p in range(2)]
        ident_made, iota_made, pool_step = sem("ident_made"), sem("iota_made"), sem("pool_step")
        dve_step = sem("dve_step")
        masks_made, gauss_arg, gauss_made = sem("masks_made"), sem("gauss_arg"), sem("gauss_made")
        waenc_ps, waenc_made = sem("waenc_ps"), sem("waenc_made")
        var_made, rstd_made = sem("var_made"), sem("rstd_made")
        hn_made, hnT_ps, hnT_made = sem("hn_made"), sem("hnT_ps"), sem("hnT_made")
        score_ps, smax_made, sexp_made = sem("score_ps"), sem("smax_made"), sem("sexp_made")
        al_made, alT_ps, alT_made = sem("al_made"), sem("alT_ps"), sem("alT_made")
        cx_ps, cx_made, co_ps, tanh_made = sem("cx_ps"), sem("cx_made"), sem("co_ps"), sem("tanh_made")
        rh_ps, rh_made, rhT_ps, rhT_made, lg_ps = (sem("rh_ps"), sem("rh_made"), sem("rhT_ps"),
                                                   sem("rhT_made"), sem("lg_ps"))
        lsub_made, lexp_made, gt_made, gT_ps, gT_made, ob_ps, ob_added = (
            sem("lsub_made"), sem("lexp_made"), sem("gt_made"), sem("gT_ps"), sem("gT_made"),
            sem("ob_ps"), sem("ob_added"))
        xT_kept = sem("xT_kept")
        s_ps, max_made, t_ps, exp_made = sem("s_ps"), sem("max_made"), sem("t_ps"), sem("exp_made")
        pv_ps, oun_made = sem("pv_ps"), sem("oun_made")
        misc_ps = [sem("miscA_ps"), sem("miscB_ps")]
        misc_free = [sem("miscA_free"), sem("miscB_free")]
        mhl_made = sem("mhl_made")
        t1_ps, onm_made, t2_ps, onT_made = sem("t1_ps"), sem("onm_made"), sem("t2_ps"), sem("onT_made")
        hi_made, mid_made, rest_made = sem("hi_made"), sem("mid_made"), sem("rest_made")
        split_made = sem("split_made")

        ROW = [("v", 0, 0), ("m", 1, 1),
               ("m", 2, 0), ("k", 0, 1), ("q", 0, 0), ("k", 1, 1), ("q", 1, 0),
               ("m", 3, 1), ("k", 2, 0), ("q", 2, 1), ("k", 3, 0), ("q", 3, 1),
               ("m", 0, 0), ("pq", 0, 1), ("pk", 0, 0), ("o", 0, 1)]
        AHEAD = {"pq": 2, "pk": 2, "v": 1, "k": 1, "q": 1}
        BEFORE = ([("pq", 0, -2), ("pk", 0, -2), ("v", 0, -1)]
                  + [(w, g, -1) for g in range(NG) for w in "kq"] + [("pq", 0, -1), ("pk", 0, -1), ("m", 0, -1)])
        bank_of = {(w, g): b for w, g, b in ROW}
        order_of = {(w, g): [e[:2] for e in ROW if e[2] == b].index((w, g)) for w, g, b in ROW}
        per_row = [sum(b == n for _, _, b in ROW) for n in range(2)]
        use_before, used = {}, [0, 0]
        for w, g, row in BEFORE:
            use_before[(w, g, row)] = used[bank_of[(w, g)]]
            used[bank_of[(w, g)]] += 1

        def use(what, g, u):
            row = u - (1 if what == "m" and g == 0 else AHEAD.get(what, 0))
            b = bank_of[(what, g)]
            if isinstance(row, int) and row < 0:
                return b, use_before[(what, g, row)]
            return b, row * per_row[b] + (used[b] + order_of[(what, g)])

        def bank_written(eng, what, g, u):
            b, n = use(what, g, u)
            eng.wait_ge(misc_ps[b], n + 1)
            return psM[b], misc_free[b]

        def open_bank(pe, what, g, u):
            b, n = use(what, g, u)
            if not (isinstance(n, int) and n == 0):
                pe.wait_ge(misc_free[b], n)
            return psM[b], misc_ps[b]

        def emptied(eng, what, g, u):
            b, n = use(what, g, u)
            eng.wait_ge(misc_free[b], n + 1)

        PACKED = ((q32, qpack, 1), (k32, kpack, 0))

        def slots(pack, which, m):
            at = [n for n, s in enumerate(SLOTS) if s[which] == m]
            runs = [at] if len(at) < 3 or at[1] - at[0] == at[2] - at[1] else [at[:2], at[2:]]
            views = []
            for a in runs:
                width = D * (a[1] - a[0]) if len(a) > 1 else D
                v = pack[:, :, D * a[0]:D * a[0] + width * len(a)]
                views.append(v.rearrange("p n (c r) -> p n c r", c=len(a))[:, :, :, 0:D])
            return views

        def spread(copy, pack, which, m, src):
            for v in slots(pack, which, m):
                last = copy(v, src[:].unsqueeze(2).to_broadcast([P, TT * H, v.shape[2], D]))
            return last

        S_AHEAD = [(2, 0), (3, 0), (0, 1), (1, 1)]

        block = st.enter_context(nc.Block())

        carried = [0]

        def apart(eng):
            carried[0] += 1
            c = carried[0] % 8
            if eng.engine == nc.vector.engine:
                eng.memset(carry[:, c:c + 1], 0.0)
            else:
                eng.tensor_tensor(carry[:, 8 + c:9 + c], mhalf[:, 0:1], mhalf[:, 0:1], ALU.mult)

        @block.sync
        def _(sp):
            sp.dma_start(acc[:], x.rearrange("b (t p) e -> p (b t) e", p=P)).then_inc(x_in, 16)
            sp.dma_start(pt[:], p_t.partition_broadcast(P)).then_inc(bc_in, 16)
            sp.dma_start(len_i[:], src_len.partition_broadcast(P)).then_inc(bc_in, 16)
            for dst, src in ((encT, ctx_t.rearrange("(k p) n -> p k n", p=P)),
                             (wa, waT.rearrange("(k p) n -> p k n", p=P)),
                             (wc, wcT.rearrange("(k p) n -> p k n", p=P)),
                             (rw1, rw1T.rearrange("(k p) n -> p k n", p=P)),
                             (rw2, rw2T), (obr, ob),
                             (rb1_b, rb1.partition_broadcast(P)), (lng_b, ln_g.partition_broadcast(P)),
                             (lnb_b, ln_b.partition_broadcast(P)), (rb2_b, rb2.partition_broadcast(P))):
                sp.dma_start(dst[:], src).then_inc(const_in, 16)
            sp.dma_start(enc[:], ctx_e[0]).then_inc(enc_in, 16)
            with sp.Fori(1, B) as b:
                sp.wait_ge(cx_ps, b)
                sp.dma_start(enc[:], ctx_e[b]).then_inc(enc_in, 16)

            loads = [0]

            def load_qkv(p, jo):
                e = 2 * jo + p
                for n, (w, bias) in enumerate(((qwT, qb), (kwT, kb), (vwT, vb))):
                    sp.dma_start(wqkv[p][:, n], w[e].rearrange("(k p) o -> p k o", p=P)).then_inc(w_in, 16)
                    sp.dma_start(bqkv[p][:, n], bias[e].partition_broadcast(P)).then_inc(w_in, 16)
                loads[0] += 6 * 16
                sp.wait_ge(w_in, loads[0])

            def load_o(p, jo):
                sp.dma_start(wo[p][:], owT[2 * jo + p].rearrange("(k p) o -> p k o", p=P)).then_inc(wo_in, 16)

            def load_x(p, b):
                sp.dma_start(xs[p][:], xT[:, b]).then_inc(xs_in[p], 16)

            def send_max(p, g, u):
                emptied(sp, "m", g, u)
                n = 4 * u + g
                if not (isinstance(n, int) and n == 0):
                    sp.wait_ge(mrow_in, 16 * n)
                sp.dma_start(Qp[p][KR:KM, G * g:G * g + G, :], mT[g % 2][:]).then_inc(mrow_in, 16)

            for p in range(2):
                load_qkv(p, 0)
                load_o(p, 0)
            sp.wait_ge(wo_in, 32)
            sp.wait_ge(xT_kept, B)
            load_x(0, 0)
            load_x(1, 0)
            send_max(0, 0, 0)

            def row(jo, b, p):
                u = 2 * b + (2 * B * jo + p)
                send_max(p, 1, u)
                last = isinstance(b, int) and b == B - 1
                if last and jo + 1 < NJ:
                    load_qkv(p, jo + 1)
                load_x(p, 0 if last else b + 1)
                send_max(p, 2, u)
                send_max(p, 3, u)
                send_max(1 - p, 0, u + 1)

            for jo in range(NJ):
                for p in range(2):
                    row(jo, 0, p)
                with sp.Fori(1, B - 1) as b:
                    for p in range(2):
                        row(jo, b, p)
                for p in range(2):
                    row(jo, B - 1, p)
                    if jo + 1 < NJ:
                        bank, n = use("o", 0, 2 * B * (jo + 1) - 2 + p)
                        sp.wait_ge(misc_ps[bank], n + 1)
                        load_o(p, jo + 1)
                        if p == 1:
                            sp.wait_ge(wo_in, 32 * (jo + 2))
            emptied(sp, "o", 0, NE * B - 1)
            sp.dma_start(out.rearrange("b (t p) e -> p (b t) e", p=P), acc[:]).then_inc(stored, 16)
            sp.wait_ge(stored, 16)
            for p in range(2):
                sp.wait_ge(xs_in[p], 8 * NE * B + 16)
            sp.wait_ge(mrow_in, 16 * (4 * NE * B + 1))

        @block.gpsimd
        def _(pool):
            own = Step(pool, pool_step)
            own.begin(0, 3)
            own(pool.memset(ident[:], 0.0))
            own(pool.affine_select(out=ident[:], in_=ident[:], compare_op=ALU.not_equal, fill=1.0, base=0,
                                   pattern=[[-1, P]], channel_multiplier=1))
            pool.tensor_copy(ident_bf[:], ident[:]).then_inc(ident_made, 1)
            pool.iota(idx[:], pattern=[[1, L]], base=0, channel_multiplier=0,
                      allow_small_or_imprecise_dtypes=True).then_inc(iota_made, 1)
            pool.iota(rank[:], pattern=[[-1, NE]], base=NE, channel_multiplier=0,
                      allow_small_or_imprecise_dtypes=True).then_inc(iota_made, 1)
            pool.memset(kpack[:, :, KR:KM], 1.0)
            for p in range(2):
                pool.memset(vaug[p][:, :, :, D:V1], 1.0)
            own(pool.memset(mhalf[:], -0.5))
            own.end(1)
            with pool.Fori(0, B) as b:
                for n in range(3):
                    pool.wait_ge(var_made, 3 * b + (n + 1))
                    pool.tensor_tensor(rstd[:], veps[:], mhalf[:], ALU.pow).then_inc(rstd_made, 1)
                    if n == 1:
                        pool.wait_ge(hnT_made, 2 * b + 2)
                        apart(pool)
                        pool.tensor_copy(xT[:, b], hnT[:]).then_inc(xT_kept, 1)

            def unit(u):
                for n, (x32, pack, which) in enumerate(PACKED):
                    pool.wait_ge(hi_made, 2 * u + n + 1)
                    pool.tensor_tensor(rest[n][:], x32[:], slots(pack, which, 0)[0][:, :, 0, :],
                                       ALU.subtract).then_inc(rest_made, 1)
                for n, (x32, pack, which) in enumerate(PACKED):
                    pool.wait_ge(mid_made, 2 * u + n + 1)
                    pool.tensor_tensor(slots(pack, which, 2)[0][:, :, 0, :], rest[n][:],
                                       slots(pack, which, 1)[0][:, :, 0, :], ALU.subtract).then_inc(split_made, 1)

            for u in range(2):
                unit(u)
            with pool.Fori(2, NE * B + 1) as u:
                unit(u)

        @block.tensor
        def _(pe):
            pe.wait_ge(ident_made, 1)
            pe.wait_ge(const_in, 16 * 10)
            half = B * L // 2
            for m in range(KT):
                for c in range(2):
                    for k in range(KT):
                        mm = pe.matmul(psS[0][:, 0:half] if (m, c) == (0, 0) else
                                       [psS[1], psS[2], psT[0]][2 * m + c - 1][:, 0:half],
                                       wa[:, k, m * P:m * P + P], encT[:, k, c * half:c * half + half],
                                       start=(k == 0), stop=(k == KT - 1))
                    mm.then_inc(waenc_ps, 1)
            pe.wait_ge(waenc_made, 4)

            with pe.Fori(0, B) as b:
                def turn(ps):
                    for k in range(KT):
                        for t in range(TT):
                            mm = pe.transpose(ps[:, k * S + t * P:k * S + t * P + P],
                                              hn[:, t, k * P:k * P + P], ident[:])
                    mm.then_inc(hnT_ps, 1)

                pe.wait_ge(hn_made, 2 * b + 1)
                turn(psS[0])
                pe.wait_ge(hnT_made, 2 * b + 1)
                for t in range(TT):
                    for k in range(KT):
                        mm = pe.matmul(psS[1][:, t * L:t * L + L], hnT[:, k, t * P:t * P + P],
                                       waenc[:, k, bass.ds(b * L, L)], start=(k == 0), stop=(k == KT - 1))
                mm.then_inc(score_ps, 1)
                pe.wait_ge(al_made, b + 1)
                for t in range(TT):
                    mm = pe.transpose(psS[2][0:L, t * P:t * P + P], al[:, t, :], ident[:])
                mm.then_inc(alT_ps, 1)
                pe.wait_ge(alT_made, b + 1)
                pe.wait_ge(enc_in, 16 * b + 16)
                for k in range(KT):
                    mm = pe.matmul(psT[0][:, k * S:k * S + S], enc[:, k * P:k * P + P], alT[:],
                                   start=True, stop=True)
                mm.then_inc(cx_ps, 1)
                pe.wait_ge(cx_made, b + 1)
                for t in range(TT):
                    for k in range(2 * KT):
                        src = cxT if k < KT else hnT
                        mm = pe.matmul(psT[1][:, t * E:t * E + E], src[:, k % KT, t * P:t * P + P], wc[:, k, :],
                                       start=(k == 0), stop=(k == 2 * KT - 1))
                mm.then_inc(co_ps, 1)
                pe.wait_ge(hn_made, 2 * b + 2)
                turn(psS[0])
                pe.wait_ge(hnT_made, 2 * b + 2)
                for t in range(TT):
                    for k in range(KT):
                        mm = pe.matmul(psS[1][:, t * R:t * R + R], hnT[:, k, t * P:t * P + P], rw1[:, k, :],
                                       start=(k == 0), stop=(k == KT - 1))
                mm.then_inc(rh_ps, 1)
                pe.wait_ge(rh_made, b + 1)
                for t in range(TT):
                    mm = pe.transpose(psS[2][:, t * P:t * P + P], rh[:, t, :], ident[:])
                mm.then_inc(rhT_ps, 1)
                pe.wait_ge(rhT_made, b + 1)
                for t in range(TT):
                    mm = pe.matmul(psV[:, t * NE:t * NE + NE], rhT[:, t * P:t * P + P], rw2[:],
                                   start=True, stop=True)
                mm.then_inc(lg_ps, 1)

            pe.wait_ge(gt_made, 1)
            banks = [psS[0], psS[1], psS[2], psT[0]]
            for t in range(NT):
                mm = pe.transpose(banks[t // 4][0:NE, (t % 4) * P:(t % 4) * P + P], gt[:, t, :], ident[:])
            mm.then_inc(gT_ps, 1)
            pe.wait_ge(gT_made, 1)
            for b in range(B):
                if b > 1:
                    pe.wait_ge(ob_added, b - 1)
                for t in range(TT):
                    mm = pe.matmul(psM[b % 2][:, t * E:t * E + E], gT[:, TT * b + t, :], obr[:],
                                   start=True, stop=True)
                mm.then_inc(ob_ps, 1)
            pe.wait_ge(ob_added, B)

            def project(what, n, p, u, tiles=range(TT)):
                for t in tiles:
                    if t == 0:
                        open_bank(pe, what, 0, u)
                    b, _ = use(what, 0, u)
                    for k in range(KT):
                        mm = pe.matmul(psM[b][:, t * E:t * E + E], xs[p][:, k, t * P:t * P + P],
                                       wqkv[p][:, n, k, :], start=(k == 0), stop=(k == KT - 1))
                    if t == TT - 1:
                        mm.then_inc(misc_ps[b], 1)

            def pack(what, g, u):
                src, rows = (kpack, KM) if what == "k" else (qpack, KR)
                pe.wait_ge(split_made, 2 * u + (2 if what == "k" else 1))
                ps, written = open_bank(pe, what, g, u)
                for h in range(G):
                    for t in range(TT):
                        c = h * S + t * P
                        mm = pe.transpose(ps[:].bitcast(BF16)[0:rows, c:c + P], src[:, t * H + G * g + h, :],
                                          ident_bf[:])
                mm.then_inc(written, 1)

            def turn_max(g, u):
                pe.wait_ge(mhl_made, 4 * u + g + 1)
                ps, written = open_bank(pe, "m", g, u)
                for t in range(TT):
                    mm = pe.transpose(ps[:].bitcast(BF16)[0:2 * G, t * P:t * P + P], mhl[g % 2][:, t, :], ident_bf[:])
                mm.then_inc(written, 1)

            def scores(p, g, j, u):
                h = G * g + j
                if j == 0 and g < 2:
                    emptied(pe, "k", g, u)
                    emptied(pe, "q", g, u)
                n = H * u + h
                back = BACK[j]
                if not (isinstance(n, int) and n < back):
                    pe.wait_ge(max_made, n - back + 1)
                for t in range(TT):
                    mm = pe.matmul(psS[S_BANK[j]][:, t * S:t * S + S], Qp[p][0:KR, h, t * P:t * P + P],
                                   Kp[p][0:KR, h, :], start=True, stop=True)
                mm.then_inc(s_ps, 1)

            def scores_T(p, h, u):
                for k in range(TT):
                    mm = pe.matmul(psT[h % 2][:, k * S:k * S + S], Kp[p][0:KM, h, k * P:k * P + P],
                                   Qp[p][0:KM, h, :], start=True, stop=True)
                mm.then_inc(t_ps, 1)

            def values(p, h, u):
                g, j = h // G, h % G
                if j == 0 and g > 0:
                    pe.wait_ge(oun_made, 4 * u + g)
                pe.wait_ge(exp_made, 16 * u + h + 1)
                for k in range(TT):
                    mm = pe.matmul(psV[32 * j:32 * j + V1, (g % 2) * S:(g % 2) * S + S],
                                   vaug[p][:, k, h, :], pexp[h % NP_][:, k, :],
                                   start=(k == 0), stop=(k == TT - 1))
                if j == G - 1:
                    mm.then_inc(pv_ps, 1)

            pe.wait_ge(xs_in[0], 16)
            project("pq", 0, 0, 0)
            project("pk", 1, 0, 0)
            project("v", 2, 0, 0)
            for g in range(NG):
                pack("k", g, 0)
                pack("q", g, 0)
            pe.wait_ge(xs_in[1], 16)
            project("pq", 0, 1, 1)
            project("pk", 1, 1, 1)
            for j in range(G):
                scores(0, 0, j, 0)
            turn_max(0, 0)
            for j in range(G):
                scores(0, 1, j, 0)

            def row(u, p):
                for g in range(NG):
                    sg, du = S_AHEAD[g]
                    su, spar = u + du, (p + du) % 2
                    pe.wait_ge(mrow_in, 64 * u + 16 * (g + 1))
                    for j in range(G):
                        scores(spar, sg, j, su)
                        h = G * g + j
                        scores_T(p, h, u)
                        if j > 0:
                            values(p, h - 1, u)
                        if j == 1:
                            mg, md = [(1, 0), (2, 0), (3, 0), (0, 1)][g]
                            turn_max(mg, u + md)
                        if j == 2:
                            if g == 0:
                                project("v", 2, 1 - p, u + 1)
                            elif g < 3:
                                pack("k", 2 * g - 2, u + 1)
                                pack("q", 2 * g - 2, u + 1)
                    if g in (1, 2):
                        pack("k", 2 * g - 1, u + 1)
                        pack("q", 2 * g - 1, u + 1)
                    values(p, G * g + G - 1, u)
                pe.wait_ge(xs_in[p], 8 * (u - p) + 32)
                project("pq", 0, p, u + 2)
                pe.wait_ge(oun_made, 4 * u + 4)
                for t in range(TT):
                    for g in range(NG):
                        mm = pe.transpose(psT[t][:, g * P:g * P + P], oun[:, g, t * P:t * P + P], ident[:])
                    mm.then_inc(t1_ps, 1)
                project("pk", 1, p, u + 2, [0])
                pe.wait_ge(onm_made, 2 * u + 2)
                for k in range(KT):
                    for t in range(TT):
                        mm = pe.transpose(psV[:, k * S + t * P:k * S + t * P + P],
                                          onm[:, t, k * H // KT:(k + 1) * H // KT, :].rearrange("p h d -> p (h d)"),
                                          ident[:])
                mm.then_inc(t2_ps, 1)
                project("pk", 1, p, u + 2, [1])
                pe.wait_ge(onT_made, u + 1)
                ps, written = open_bank(pe, "o", 0, u)
                for t in range(TT):
                    for k in range(KT):
                        mm = pe.matmul(ps[:, t * E:t * E + E], onT[:, k, t * P:t * P + P], wo[p][:, k, :],
                                       start=(k == 0), stop=(k == KT - 1))
                mm.then_inc(written, 1)

            with pe.Fori(0, NE * B // 2) as i:
                for p in range(2):
                    row(2 * i + p, p)

        @block.scalar
        def _(act):
            act.wait_ge(gauss_arg, 1)
            act.activation(gauss[:], gauss[:], ACT.Exp, scale=-1.0 / DEV_POW).then_inc(gauss_made, 1)
            half = B * L // 2
            for n in range(4):
                act.wait_ge(waenc_ps, n + 1)
                src = [psS[0], psS[1], psS[2], psT[0]][n]
                act.activation(waenc[:, n // 2, (n % 2) * half:(n % 2) * half + half], src[:, 0:half],
                               ACT.Copy).then_inc(waenc_made, 1)
            with act.Fori(0, B) as b:
                act.wait_ge(hnT_ps, 2 * b + 1)
                act.activation(hnT[:].rearrange("p k s -> p (k s)"), psS[0][:], ACT.Copy).then_inc(hnT_made, 1)
                act.wait_ge(smax_made, b + 1)
                for t in range(TT):
                    ins = act.activation(sc[:, t, :], sc[:, t, :], ACT.Exp, bias=smx[:, t:t + 1],
                                         accum_out=ssum[:, t:t + 1])
                    ins.then_inc(sexp_made, 1)
                act.wait_ge(alT_ps, b + 1)
                act.activation(alT[:], psS[2][0:L, 0:S], ACT.Copy).then_inc(alT_made, 1)
                act.wait_ge(cx_ps, b + 1)
                act.activation(cxT[:].rearrange("p k s -> p (k s)"), psT[0][:], ACT.Copy).then_inc(cx_made, 1)
                act.wait_ge(co_ps, b + 1)
                act.activation(th[:].rearrange("p k s -> p (k s)"), psT[1][:], ACT.Tanh).then_inc(tanh_made, 1)
                act.wait_ge(hnT_ps, 2 * b + 2)
                act.activation(hnT[:].rearrange("p k s -> p (k s)"), psS[0][:], ACT.Copy).then_inc(hnT_made, 1)
                act.wait_ge(rhT_ps, b + 1)
                act.activation(rhT[:], psS[2][:, 0:S], ACT.Copy).then_inc(rhT_made, 1)
            act.wait_ge(lsub_made, 1)
            act.activation(pr[:], lg[:], ACT.Exp).then_inc(lexp_made, 1)
            act.wait_ge(gT_ps, 1)
            for n in range(4):
                last = act.activation(gT[:, 4 * n:4 * n + 4, :].rearrange("p a b -> p (a b)"),
                                      [psS[0], psS[1], psS[2], psT[0]][n][0:NE, :], ACT.Copy)
            last.then_inc(gT_made, 1)

            def keep_q(p, g, u):
                ps, free = bank_written(act, "q", g, u)
                act.activation(Qp[p][0:KR, G * g:G * g + G, :].rearrange("p h s -> p (h s)"),
                               ps[:].bitcast(BF16)[0:KR, :], ACT.Copy).then_inc(free, 1)

            def keep_max(g, u):
                ps, free = bank_written(act, "m", g, u)
                act.activation(mT[g % 2][:], ps[:].bitcast(BF16)[0:2 * G, 0:S], ACT.Copy).then_inc(free, 1)

            def middle(n, u):
                act.wait_ge(rest_made, 2 * u + n + 1)
                _, pack, which = PACKED[n]
                spread(lambda o, i: act.activation(o, i, ACT.Copy), pack, which, 1,
                       rest[n]).then_inc(mid_made, 1)

            middle(0, 0)
            middle(1, 0)
            for g in range(NG):
                keep_q(0, g, 0)
            keep_max(0, 0)

            def row(u, p):
                for g in range(NG):
                    for j in range(G):
                        h = G * g + j
                        act.wait_ge(t_ps, 16 * u + h + 1)
                        n = 16 * u + h
                        act.activation(pexp[h % NP_][:].rearrange("p k s -> p (k s)"), psT[h % 2][:],
                                       ACT.Exp, scale=SCALE).then_inc(exp_made, 1)
                        if j == 1:
                            mg, md = [(1, 0), (2, 0), (3, 0), (0, 1)][g]
                            keep_max(mg, u + md)
                        if g == 0 and j in (0, 2):
                            middle(j // 2, u + 1)
                        if j == 2 and g in (1, 2):
                            keep_q(1 - p, 2 * g - 2, u + 1)
                    if g in (1, 2):
                        keep_q(1 - p, 2 * g - 1, u + 1)
                    act.wait_ge(pv_ps, 4 * u + g + 1)
                    act.activation(oun[:, g, :], psV[:, (g % 2) * S:(g % 2) * S + S], ACT.Copy).then_inc(oun_made, 1)
                act.wait_ge(t2_ps, u + 1)
                act.activation(onT[:].rearrange("p k s -> p (k s)"), psV[:], ACT.Copy).then_inc(onT_made, 1)

            with act.Fori(0, NE * B // 2) as i:
                for p in range(2):
                    row(2 * i + p, p)

        @block.vector
        def _(dve):
            own = Step(dve, dve_step)
            own.begin(0, 8)
            dve.memset(psV[:], 0.0)
            dve.wait_ge(iota_made, 2)
            dve.wait_ge(bc_in, 32)
            own(dve.tensor_scalar(w_start[:], pt[:], -WINDOW, 0.0, ALU.add, ALU.max))
            own(dve.tensor_scalar(w_end[:], pt[:], WINDOW, None, ALU.add))
            own(dve.tensor_copy(len_f[:], len_i[:]))
            own(dve.tensor_tensor(w_end[:], w_end[:], len_f[:], ALU.min))
            idx_b = idx[:].unsqueeze(1).to_broadcast([P, B, L])

            def per_batch(a):
                return a[:].unsqueeze(2).to_broadcast([P, B, L])

            own(dve.tensor_tensor(keep[:], idx_b, per_batch(w_start), ALU.is_ge))
            own(dve.tensor_tensor(keep2[:], idx_b, per_batch(w_end), ALU.is_le))
            own(dve.tensor_tensor(keep[:], keep[:], keep2[:], ALU.mult))
            dve.tensor_scalar(fill[:], keep[:], NEG, -NEG, ALU.mult, ALU.add)
            own(dve.tensor_tensor(gauss[:], idx_b, per_batch(pt), ALU.subtract))
            dve.tensor_tensor(gauss[:], gauss[:], gauss[:], ALU.mult).then_inc(gauss_arg, 1)
            own.end(1)
            dve.wait_ge(gauss_made, 1)
            dve.wait_ge(x_in, 16)
            dve.wait_ge(const_in, 160)

            def stats_of(tiles, n, b):
                for t in range(TT):
                    last = dve.bn_stats(stats[:, t, :], tiles[t])
                own(last, apart)
                for t in range(TT):
                    last = dve.bn_aggr(mv[:, t, :], stats[:, t, :])
                own(last)
                dve.tensor_scalar(veps[:], mv[:, :, 1], EPS, None, ALU.add).then_inc(var_made, 1)
                dve.wait_ge(rstd_made, 3 * b + (n + 1))

            def normalise(dst, tiles):
                for t in range(TT):
                    last = dve.tensor_scalar(dst[:, t, :], tiles[t], mv[:, t, 0:1], rstd[:, t:t + 1],
                                             ALU.subtract, ALU.mult)
                return last

            with dve.Fori(0, B) as b:
                own.begin(b, 16)
                tiles = [acc[:, TT * b + t, :] for t in range(TT)]
                stats_of(tiles, 0, b)
                normalise(hn, tiles).then_inc(hn_made, 1)
                dve.wait_ge(score_ps, b + 1)
                kb_ = keep[:, bass.ds(b, 1), :].to_broadcast([P, TT, L])
                fb_ = fill[:, bass.ds(b, 1), :].to_broadcast([P, TT, L])
                own(dve.tensor_tensor(sc[:], psS[1][:, 0:TT * L].rearrange("p (t l) -> p t l", t=TT), kb_, ALU.mult))
                own(dve.tensor_tensor(sc[:], sc[:], fb_, ALU.add))
                dve.tensor_reduce(smx[:], sc[:], AX.X, ALU.max, negate=True).then_inc(smax_made, 1)
                dve.wait_ge(sexp_made, TT * b + TT)
                own(dve.reciprocal(ssum[:], ssum[:]))
                own(dve.tensor_tensor(sc[:], sc[:], ssum[:].unsqueeze(2).to_broadcast([P, TT, L]), ALU.mult))
                dve.tensor_tensor(al[:], sc[:], gauss[:, bass.ds(b, 1), :].to_broadcast([P, TT, L]),
                                  ALU.mult).then_inc(al_made, 1)
                dve.wait_ge(tanh_made, b + 1)
                own(dve.tensor_tensor(acc[:, bass.ds(TT * b, TT), :], acc[:, bass.ds(TT * b, TT), :], th[:], ALU.add),
                    apart)
                stats_of(tiles, 1, b)
                normalise(hn, tiles).then_inc(hn_made, 1)
                dve.wait_ge(rh_ps, b + 1)
                rtiles = [rh[:, t, :] for t in range(TT)]
                own(dve.tensor_tensor(rh[:], psS[1][:, 0:TT * R].rearrange("p (t r) -> p t r", t=TT),
                                      rb1_b[:].unsqueeze(1).to_broadcast([P, TT, R]), ALU.add))
                stats_of(rtiles, 2, b)
                own(normalise(rh, rtiles))
                own(dve.tensor_tensor(rh[:], rh[:], lng_b[:].unsqueeze(1).to_broadcast([P, TT, R]), ALU.mult))
                own(dve.tensor_tensor(rh[:], rh[:], lnb_b[:].unsqueeze(1).to_broadcast([P, TT, R]), ALU.add))
                dve.tensor_scalar(rh[:], rh[:], 0.0, None, ALU.max).then_inc(rh_made, 1)
                dve.wait_ge(lg_ps, b + 1)
                own(dve.tensor_tensor(lg[:, bass.ds(TT * b, TT), :],
                                      psV[:, 0:TT * NE].rearrange("p (t e) -> p t e", t=TT),
                                      rb2_b[:].unsqueeze(1).to_broadcast([P, TT, NE]), ALU.add))
            own.end(B)

            def per_token(a):
                return a[:].unsqueeze(2).to_broadcast([P, NT, NE])

            rank_b = rank[:].unsqueeze(1).to_broadcast([P, NT, NE])
            own.begin(0, 18)
            own(dve.tensor_reduce(r1[:], lg[:], AX.X, ALU.max))
            dve.tensor_tensor(lg[:], lg[:], per_token(r1), ALU.subtract).then_inc(lsub_made, 1)
            dve.wait_ge(lexp_made, 1)
            own(dve.reduce_sum(r2[:], pr[:], AX.X))
            own(dve.reciprocal(r2[:], r2[:]))
            own(dve.tensor_tensor(pr[:], pr[:], per_token(r2), ALU.mult))

            def pick(src, top, one_hot):
                own(dve.tensor_reduce(top[:], src[:], AX.X, ALU.max))
                own(dve.tensor_tensor(eq[:], src[:], per_token(top), ALU.is_equal))
                own(dve.tensor_tensor(eq[:], eq[:], rank_b, ALU.mult))
                own(dve.tensor_reduce(r3[:], eq[:], AX.X, ALU.max))
                own(dve.tensor_tensor(one_hot[:], eq[:], per_token(r3), ALU.is_equal))

            pick(pr, r1, oh1)
            own(dve.scalar_tensor_tensor(pr2[:].rearrange("p a b -> p (a b)"), oh1[:].rearrange("p a b -> p (a b)"),
                                         -2.0, pr[:].rearrange("p a b -> p (a b)"), ALU.mult, ALU.add))
            pick(pr2, r2, oh2)
            own(dve.tensor_tensor(r1[:], r1[:], r2[:], ALU.add))
            own(dve.reciprocal(r1[:], r1[:]))
            own(dve.tensor_tensor(oh1[:], oh1[:], oh2[:], ALU.add))
            own.end(1)
            own.begin(0, 2)
            own(dve.tensor_tensor(oh1[:], oh1[:], pr[:], ALU.mult))
            dve.tensor_tensor(gt[:], oh1[:], per_token(r1), ALU.mult).then_inc(gt_made, 1)
            dve.wait_ge(gt_made, 1)
            own(dve.tensor_copy(gates[:].rearrange("p (e t) -> p t e", e=NE), gt[:]))
            own.end(1)
            for b in range(B):
                dve.wait_ge(ob_ps, b + 1)
                a = acc[:, TT * b:TT * b + TT, :]
                dve.tensor_tensor(a, a, psM[b % 2][:].rearrange("p (t e) -> p t e", t=TT),
                                  ALU.add).then_inc(ob_added, 1)

            def keep_32(what, n, dst, p, u):
                ps, free = bank_written(dve, what, 0, u)
                if not (isinstance(u, int) and u == 0):
                    dve.wait_ge(split_made, 2 * u)
                dve.tensor_tensor(dst[:].rearrange("p (t h) d -> p t (h d)", t=TT),
                                  ps[:].rearrange("p (t e) -> p t e", t=TT),
                                  bqkv[p][:, n, :].unsqueeze(1).to_broadcast([P, TT, E]),
                                  ALU.add).then_inc(free, 1)
                emptied(dve, what, 0, u)
                _, pack, which = PACKED[n]
                spread(dve.tensor_copy, pack, which, 0, dst).then_inc(hi_made, 1)

            def keep_v(p, u):
                ps, free = bank_written(dve, "v", 0, u)
                dve.tensor_tensor(vaug[p][:, :, :, 0:D], ps[:].rearrange("p (t h d) -> p t h d", t=TT, h=H),
                                  bqkv[p][:, 2, :].rearrange("p (h d) -> p h d", h=H).unsqueeze(1)
                                  .to_broadcast([P, TT, H, D]), ALU.add).then_inc(free, 1)

            def keep_k(p, g, u):
                ps, free = bank_written(dve, "k", g, u)
                dve.tensor_copy(Kp[p][0:KM, G * g:G * g + G, :].rearrange("p h s -> p (h s)"),
                                ps[:].bitcast(BF16)[0:KM, :]).then_inc(free, 1)

            def head_max(g, j, u):
                dve.wait_ge(s_ps, 16 * u + G * g + j + 1)
                dve.tensor_reduce(negm[g % 2][:, :, j], psS[S_BANK[j]][:].rearrange("p (t s) -> p t s", t=TT), AX.X,
                                  ALU.max, negate=True).then_inc(max_made, 1)

            def split_max(g, u):
                dve.wait_ge(max_made, 16 * u + G * g + G)
                own(dve.tensor_copy(mhl[g % 2][:, :, 0:G], negm[g % 2][:]))
                dve.tensor_tensor(mhl[g % 2][:, :, G:2 * G], negm[g % 2][:], mhl[g % 2][:, :, 0:G],
                                  ALU.subtract).then_inc(mhl_made, 1)

            own.begin(0, 2)
            keep_32("pq", 0, q32, 0, 0)
            keep_32("pk", 1, k32, 0, 0)
            keep_v(0, 0)
            for g in range(NG):
                keep_k(0, g, 0)
            keep_32("pq", 0, q32, 1, 1)
            keep_32("pk", 1, k32, 1, 1)
            for g in range(2):
                for j in range(G):
                    head_max(g, j, 0)
                split_max(g, 0)
            own.end(1)

            def row(u, p, e, tile):
                for g in range(NG):
                    sg, du = S_AHEAD[g]
                    for j in range(G):
                        head_max(sg, j, u + du)
                        if j == 2:
                            if g == 0:
                                keep_v(1 - p, u + 1)
                            elif g < 3:
                                keep_k(1 - p, 2 * g - 2, u + 1)
                    split_max(sg, u + du)
                    if g in (1, 2):
                        keep_k(1 - p, 2 * g - 1, u + 1)
                keep_32("pq", 0, q32, p, u + 2)
                for t in range(TT):
                    dve.wait_ge(t1_ps, 2 * u + t + 1)
                    heads = psT[t][:].rearrange("p (h c) -> p h c", h=H)
                    own(dve.reciprocal(rcp[:, t, :], heads[:, :, D]))
                    own(dve.tensor_scalar(rgt[:, t, :], rcp[:, t, :], gates[:, bass.ds(e * NT + tile + t, 1)], None, ALU.mult))
                    dve.tensor_tensor(onm[:, t], heads[:, :, 0:D],
                                      rgt[:, t, :].unsqueeze(2).to_broadcast([P, H, D]), ALU.mult).then_inc(onm_made, 1)
                keep_32("pk", 1, k32, p, u + 2)
                ps, free = bank_written(dve, "o", 0, u)
                a = acc[:, bass.ds(tile, TT), :]
                dve.tensor_tensor(a, a, ps[:].rearrange("p (t e) -> p t e", t=TT), ALU.add).then_inc(free, 1)

            with dve.Fori(0, NJ) as jo:
                with dve.Fori(0, B) as b:
                    own.begin(jo * B + b, 2 * (NG + 2 * TT))
                    for p in range(2):
                        row(2 * B * jo + 2 * b + p, p, 2 * jo + p, TT * b)
            own.end(NJ * B)


def kernel(**inputs):
    import numpy as np
    import concourse.bacc as bacc
    from concourse.bass_utils import run_bass_kernel_spmd

    def turned(a):
        return np.ascontiguousarray(np.swapaxes(a, -1, -2))

    i = {k: np.asarray(v) for k, v in inputs.items()}
    f = {n: i["L0_ffn_" + n] for n in ("rW1", "rb1", "ln_g", "ln_b", "rW2", "rb2", "qW", "qb", "kW", "kb",
                                       "vW", "vb", "oW", "ob")}
    ctx = i["ctx_1024"]
    arrays = {
        "x": i["x"], "ctx_e": ctx,
        "ctx_t": np.ascontiguousarray(ctx.transpose(2, 0, 1).reshape(ctx.shape[2], -1)),
        "p_t": i["condB_pt"], "src_len": i["_lenS2"],
        "waT": turned(i["L0_xcond_W_a"]), "wcT": turned(i["L0_xcond_W_c"]),
        "rw1T": turned(f["rW1"]), "rb1": f["rb1"], "ln_g": f["ln_g"], "ln_b": f["ln_b"],
        "rw2T": turned(f["rW2"]), "rb2": f["rb2"],
        "qwT": turned(f["qW"]), "qb": f["qb"], "kwT": turned(f["kW"]), "kb": f["kb"],
        "vwT": turned(f["vW"]), "vb": f["vb"], "owT": turned(f["oW"]), "ob": f["ob"],
    }
    nc = bacc.Bacc("TRN2", target_bir_lowering=False, num_devices=1)
    args = {n: nc.dram_tensor("in_" + n, a.shape, mybir.dt.from_np(a.dtype), kind="ExternalInput").ap()
            for n, a in arrays.items()}
    out = nc.dram_tensor("out_0", i["x"].shape, F32, kind="ExternalOutput").ap()
    pixart_block(nc, out=out, **args)
    r = run_bass_kernel_spmd(nc, [{"in_" + n: np.ascontiguousarray(a) for n, a in arrays.items()}], core_ids=[0])
    return r.results[0]["out_0"]
```

```python
from contextlib import ExitStack

import concourse.bass as bass
from concourse import mybir

ALU = mybir.AluOpType
ACT = mybir.ActivationFunctionType
AX = mybir.AxisListType
F32 = mybir.dt.float32
BF16 = mybir.dt.bfloat16
I32 = mybir.dt.int32


class Step:

    def __init__(self, eng, sem):
        self.eng, self.sem, self.done = eng, sem, 0

    def begin(self, turn, per):
        self.turn, self.per, self.local = turn, per, 0

    def __call__(self, ins, apart=None):
        self.local += 1
        ins.then_inc(self.sem, 1)
        self.eng.wait_ge(self.sem, self.turn * self.per + (self.done + self.local))
        if apart:
            apart(self.eng)

    def end(self, turns):
        assert self.local == self.per, self.local
        self.done += turns * self.per


def pixart_block(nc, x, ctx_e, ctx_t, p_t, src_len, waT, wcT, rw1T, rb1, ln_g, ln_b, rw2T, rb2,
                 qwT, kwT, qkb, vwT, vb, owT, ob, out):
    B, S, E = x.shape
    L = ctx_e.shape[1]
    NE = qwT.shape[0]
    R = rw1T.shape[1]
    H = 16
    D = E // H
    P = 128
    TT = S // P
    KT = E // P
    NT = B * TT
    G = 4
    NG = H // G
    V1 = D + 1
    KR = 6 * D
    KM = KR + 2
    SCALE = float(D) ** -0.5
    WINDOW, DEV_POW, NEG, EPS = 16.0, 128.0, 1e9, 1e-5
    assert TT == 2 and KT == 2 and NG == 4 and E == H * D and NE % 2 == 0 and R == P
    NJ = NE // 2
    HP = P // D
    PARTS = (((0, 1), 0), ((0, 1), 2), ((0,), 4), ((2,), 5)), (((0, 1, 2), 0), ((0, 1), 3), ((0,), 5))
    order = [[m for run, _ in PARTS[n] for m in run] for n in range(2)]
    assert sorted(zip(*order)) == [(0, 0), (0, 1), (0, 2), (1, 0), (1, 1), (2, 0)]

    with ExitStack() as st:
        def sb(name, shape, dt=F32):
            return st.enter_context(nc.sbuf_tensor(name, shape, dt))

        def psum(name):
            return st.enter_context(nc.psum_tensor(name, [P, 512], F32))

        def sem(name):
            return st.enter_context(nc.semaphore(name))

        acc = sb("acc", [P, NT, E])
        xT = sb("xT", [P, B, KT, S])
        gates = sb("gates", [P, NE * NT])
        ident = sb("ident", [P, P])
        ident_bf = sb("ident_bf", [P, P], BF16)
        enc = [sb(f"enc{q}", [L, E]) for q in range(2)]
        encT = sb("encT", [P, KT, B * L])
        wa = sb("wa", [P, KT, E])
        wc = sb("wc", [P, 2 * KT, E])
        waenc = sb("waenc", [P, KT, B * L])
        pt = sb("pt", [P, B])
        len_i = sb("len_i", [P, B], I32)
        len_f = sb("len_f", [P, B])
        w_start = sb("w_start", [P, B])
        w_end = sb("w_end", [P, B])
        idx = sb("idx", [P, L])
        keep = sb("keep", [P, B, L])
        keep2 = sb("keep2", [P, B, L])
        fill = sb("fill", [P, B, L])
        gauss = sb("gauss", [P, B, L])
        rw1 = sb("rw1", [P, KT, R])
        rw2 = sb("rw2", [R, NE])
        rb1_b = sb("rb1_b", [P, R])
        lng_b = sb("lng_b", [P, R])
        lnb_b = sb("lnb_b", [P, R])
        rb2_b = sb("rb2_b", [P, NE])
        obr = sb("obr", [NE, E])
        mhalf = sb("mhalf", [P, TT])
        carry = sb("carry", [P, 16])
        stats = [sb(f"stats{q}", [P, TT, 6]) for q in range(2)]
        mv = [sb(f"mv{q}", [P, TT, 2]) for q in range(2)]
        veps = [sb(f"veps{q}", [P, TT]) for q in range(2)]
        rstd = [sb(f"rstd{q}", [P, TT]) for q in range(2)]
        hn = [sb(f"hn{q}", [P, TT, E]) for q in range(2)]
        hnT = [sb(f"hnT{q}", [P, KT, S]) for q in range(2)]
        sc = [sb(f"sc{q}", [P, TT, L]) for q in range(2)]
        smx = [sb(f"smx{q}", [P, TT]) for q in range(2)]
        ssum = [sb(f"ssum{q}", [P, TT]) for q in range(2)]
        al = [sb(f"al{q}", [P, TT, L]) for q in range(2)]
        alT = [sb(f"alT{q}", [L, S]) for q in range(2)]
        cxT = [sb(f"cxT{q}", [P, KT, S]) for q in range(2)]
        th = [sb(f"th{q}", [P, TT, E]) for q in range(2)]
        rh = [sb(f"rh{q}", [P, TT, R]) for q in range(2)]
        rhT = [sb(f"rhT{q}", [P, S]) for q in range(2)]
        lg = sb("lg", [P, NT, NE])
        rank = sb("rank", [P, NE])
        pr = sb("pr", [P, NT, NE])
        pr2 = sb("pr2", [P, NT, NE])
        eq = sb("eq", [P, NT, NE])
        oh1 = sb("oh1", [P, NT, NE])
        oh2 = sb("oh2", [P, NT, NE])
        r1 = sb("r1", [P, NT])
        r2 = sb("r2", [P, NT])
        r3 = sb("r3", [P, NT])
        gt = sb("gt", [P, NT, NE])
        gT = sb("gT", [NE, NT, P])
        xs = [sb(f"xs{p}", [P, KT, S]) for p in range(2)]
        wqkv = [sb(f"wqkv{p}", [P, 3, KT, E]) for p in range(2)]
        bqk = sb("bqk", [P, 2 * NE, KT])
        bv = [sb(f"bv{p}", [P, E]) for p in range(2)]
        wo = [sb(f"wo{p}", [P, KT, E]) for p in range(2)]
        x32 = [sb(f"x32{n}", [P, KT, S]) for n in range(2)]
        rest = [sb(f"rest{n}", [P, KT, S]) for n in range(2)]
        parts = [sb(f"parts{n}", [P, 3, KT, S], BF16) for n in range(2)]
        packed = [nc.dram_tensor(f"packed{n}", (3, P, KT * S), BF16).ap() for n in range(2)]
        Qp = [sb(f"Qp{p}", [KM, H, S], BF16) for p in range(2)]
        Kp = [sb(f"Kp{p}", [KM, H, S], BF16) for p in range(2)]
        vaug = [sb(f"vaug{p}", [P, TT, H, V1]) for p in range(2)]
        negm = [sb(f"negm{p}", [P, TT, G]) for p in range(2)]
        mhl = [sb(f"mhl{p}", [P, TT, 2 * G], BF16) for p in range(2)]
        mT = [sb(f"mT{p}", [2 * G, S], BF16) for p in range(2)]
        NP_ = 4
        pexp = [sb(f"pexp{n}", [P, TT, S]) for n in range(NP_)]
        oun = sb("oun", [P, NG, S])
        rcp = sb("rcp", [P, TT, H])
        rgt = sb("rgt", [P, TT, H])
        onm = sb("onm", [P, TT, H, D])
        onT = sb("onT", [P, KT, S])

        NS = 3
        S_BANK, BACK = (0, 1, 2, 1), (4, 2, 4, 2)
        psS = [psum(f"psS{n}") for n in range(NS)]
        psT = [psum(f"psT{n}") for n in range(2)]
        psV = psum("psV")
        psM = [psum("psA"), psum("psB")]
        bank_a, bank_b, bank_c, bank_d = (psS[0], psS[1]), (psS[2], psT[0]), (psT[1], psV), (psM[0], psM[1])

        x_in, const_in, bc_in = sem("x_in"), sem("const_in"), sem("bc_in")
        enc_in = [sem(f"enc_in{q}") for q in range(2)]
        wqk_in, wv_in = [sem(f"wqk_in{p}") for p in range(2)], [sem(f"wv_in{p}") for p in range(2)]
        wo_in, mrow_in, stored = sem("wo_in"), sem("mrow_in"), sem("stored")
        xs_in = [sem(f"xs_in{p}") for p in range(2)]
        ident_made, iota_made, pool_step = sem("ident_made"), sem("iota_made"), sem("pool_step")
        dve_step = sem("dve_step")
        masks_made, gauss_arg, gauss_made = sem("masks_made"), sem("gauss_arg"), sem("gauss_made")
        waenc_ps, waenc_made = sem("waenc_ps"), sem("waenc_made")
        var_made, rstd_made = sem("var_made"), sem("rstd_made")
        hn_made, hnT_ps, hnT_made = sem("hn_made"), sem("hnT_ps"), sem("hnT_made")
        score_ps, smax_made, sexp_made = sem("score_ps"), sem("smax_made"), sem("sexp_made")
        al_made, alT_ps, alT_made = sem("al_made"), sem("alT_ps"), sem("alT_made")
        cx_ps, cx_made, co_ps, tanh_made = sem("cx_ps"), sem("cx_made"), sem("co_ps"), sem("tanh_made")
        rh_ps, rh_made, rhT_ps, rhT_made, lg_ps = (sem("rh_ps"), sem("rh_made"), sem("rhT_ps"),
                                                   sem("rhT_made"), sem("lg_ps"))
        lsub_made, lexp_made, gt_made, gT_ps, gT_made, ob_ps, ob_added = (
            sem("lsub_made"), sem("lexp_made"), sem("gt_made"), sem("gT_ps"), sem("gT_made"),
            sem("ob_ps"), sem("ob_added"))
        xT_kept = sem("xT_kept")
        s_ps, max_made, t_ps, exp_made = sem("s_ps"), sem("max_made"), sem("t_ps"), sem("exp_made")
        pv_ps, oun_made = sem("pv_ps"), sem("oun_made")
        misc_ps = [sem("miscA_ps"), sem("miscB_ps")]
        misc_free = [sem("miscA_free"), sem("miscB_free")]
        mhi_made, mhl_made = sem("mhi_made"), sem("mhl_made")
        rcp_made, rgt_made = sem("rcp_made"), sem("rgt_made")
        t1_ps, onm_made, t2_ps, onT_made = sem("t1_ps"), sem("onm_made"), sem("t2_ps"), sem("onT_made")
        hi_made, mid_made, rest_made = sem("hi_made"), sem("mid_made"), sem("rest_made")
        split_made = sem("split_made")
        parts_out, slots_in = sem("parts_out"), sem("slots_in")

        EXTRAS = [[[], [("m", 1, 1)], [("pq", 0, 0)], [("t1", 0, 1)]],
                  [[("t1", 1, 0)], [("m", 2, 1)], [("pk", 0, 0)], [("t2", 0, 1)]],
                  [[], [("m", 3, 0)], [("o", 0, 1)], []],
                  [[], [("m", 0, 0)], [("v", 0, 1)], []]]
        ROW = [e for quarter in EXTRAS for step in quarter for e in step]
        UNITS = NE * B

        def unit_of(what, g, row):
            return row + {"pq": 2, "pk": 2, "v": 1, "t1": -1, "t2": -1, "o": -1}.get(
                what, 1 if (what, g) == ("m", 0) else 0)

        BEFORE = [("pq", 0, 0), ("pk", 0, 0), ("v", 0, 0), ("pq", 0, 1), ("pk", 0, 1), ("m", 0, 0)]
        bank_of = {(w, g): b for w, g, b in ROW}
        per_row = [sum(b == n for _, _, b in ROW) for n in range(2)]
        ordinal, used = {}, [0, 0]
        for w, g, u in BEFORE + [(w, g, unit_of(w, g, row)) for row in range(UNITS + 1) for w, g, _ in ROW]:
            if 0 <= u < UNITS and (w, g, u) not in ordinal:
                ordinal[(w, g, u)] = used[bank_of[(w, g)]]
                used[bank_of[(w, g)]] += 1

        def use(what, g, u):
            b = bank_of[(what, g)]
            if isinstance(u, int):
                return b, ordinal[(what, g, u)]
            some = 4
            return b, u * per_row[b] + (ordinal[(what, g, some)] - some * per_row[b])

        def bank_written(eng, what, g, u):
            b, n = use(what, g, u)
            eng.wait_ge(misc_ps[b], n + 1)
            return psM[b], misc_free[b]

        def open_bank(pe, what, g, u):
            b, n = use(what, g, u)
            if not (isinstance(n, int) and n == 0):
                pe.wait_ge(misc_free[b], n)
            return psM[b], misc_ps[b]

        def emptied(eng, what, g, u):
            b, n = use(what, g, u)
            eng.wait_ge(misc_free[b], n + 1)

        def rows(eng, quarter):
            def row(u, p):
                for g in range(NG):
                    quarter(u, g, p)

            row(0, 0)
            with eng.Fori(0, UNITS // 2 - 2) as i:
                row(2 * i + 1, 1)
                row(2 * i + 2, 0)
            for u in range(UNITS - 3, UNITS):
                row(u, u % 2)

        def there(u):
            return not isinstance(u, int) or 0 <= u < UNITS

        MIDDLE = [(1, 0), (2, 1)]
        SLOTS_IN = 16 * sum(len(runs) for runs in PARTS)
        S_AHEAD = [(2, 0), (3, 0), (0, 1), (1, 1)]

        block = st.enter_context(nc.Block())

        carried = [0]

        def apart(eng):
            carried[0] += 1
            c = carried[0] % 8
            if eng.engine == nc.vector.engine:
                eng.memset(carry[:, c:c + 1], 0.0)
            else:
                eng.tensor_tensor(carry[:, 8 + c:9 + c], mhalf[:, 0:1], mhalf[:, 0:1], ALU.mult)

        @block.sync
        def _(sp):
            sp.dma_start(acc[:], x.rearrange("b (t p) e -> p (b t) e", p=P)).then_inc(x_in, 16)
            sp.dma_start(pt[:], p_t.partition_broadcast(P)).then_inc(bc_in, 16)
            sp.dma_start(len_i[:], src_len.partition_broadcast(P)).then_inc(bc_in, 16)
            for dst, src in ((encT, ctx_t.rearrange("(k p) n -> p k n", p=P)),
                             (wa, waT.rearrange("(k p) n -> p k n", p=P)),
                             (wc, wcT.rearrange("(k p) n -> p k n", p=P)),
                             (rw1, rw1T.rearrange("(k p) n -> p k n", p=P)),
                             (rw2, rw2T), (obr, ob), (bqk, qkb),
                             (rb1_b, rb1.partition_broadcast(P)), (lng_b, ln_g.partition_broadcast(P)),
                             (lnb_b, ln_b.partition_broadcast(P)), (rb2_b, rb2.partition_broadcast(P))):
                sp.dma_start(dst[:], src).then_inc(const_in, 16)
            for q in range(2):
                sp.dma_start(enc[q][:], ctx_e[q]).then_inc(enc_in[q], 16)
            with sp.Fori(1, B // 2) as i:
                for q in range(2):
                    sp.wait_ge(cx_ps, 2 * i + (q - 1))
                    sp.dma_start(enc[q][:], ctx_e[2 * i + q]).then_inc(enc_in[q], 16)

            def load_qk(p, jo):
                for n, w in enumerate((qwT, kwT)):
                    sp.dma_start(wqkv[p][:, n], w[2 * jo + p].rearrange("(k p) o -> p k o", p=P)).then_inc(wqk_in[p], 16)

            def load_v(p, jo):
                e = 2 * jo + p
                sp.dma_start(wqkv[p][:, 2], vwT[e].rearrange("(k p) o -> p k o", p=P)).then_inc(wv_in[p], 16)
                sp.dma_start(bv[p][:], vb[e].partition_broadcast(P)).then_inc(wv_in[p], 16)

            def load_o(p, jo):
                sp.dma_start(wo[p][:], owT[2 * jo + p].rearrange("(k p) o -> p k o", p=P)).then_inc(wo_in, 16)

            def load_x(p, b):
                sp.dma_start(xs[p][:], xT[:, b]).then_inc(xs_in[p], 16)

            def send_max(p, g, u):
                emptied(sp, "m", g, u)
                n = 4 * u + g
                if not (isinstance(n, int) and n == 0):
                    sp.wait_ge(mrow_in, 16 * n)
                sp.dma_start(Qp[p][KR:KM, G * g:G * g + G, :], mT[g % 2][:]).then_inc(mrow_in, 16)

            def parts_to_dram(n, low, u):
                if low:
                    sp.wait_ge(split_made, 2 * u + n + 1)
                    sp.dma_start(packed[n][1:3].rearrange("m p f -> p m f"),
                                 parts[n][:, 1:3].rearrange("p m k s -> p m (k s)")).then_inc(parts_out, 16)
                else:
                    sp.wait_ge(hi_made, 2 * u + n + 1)
                    sp.dma_start(packed[n][0], parts[n][:, 0].rearrange("p k s -> p (k s)")).then_inc(parts_out, 16)

            def slots_from_dram(n, p, runs):
                for run, at in PARTS[n][runs]:
                    sp.dma_start((Qp, Kp)[n][p][D * at:D * at + D * len(run)].rearrange("p h s -> p (h s)"),
                                 packed[n][run[0]:run[0] + len(run)].rearrange("m (r h) f -> (m r) (h f)", r=D)
                                 ).then_inc(slots_in, 16)

            def before_slots(u):
                sp.wait_ge(parts_out, 64 * u + 64)
                if not (isinstance(u, int) and u < 2):
                    sp.wait_ge(t_ps, H * u - H)

            for p in range(2):
                load_qk(p, 0)
                load_v(p, 0)
                load_o(p, 0)
            sp.wait_ge(wo_in, 32)
            sp.wait_ge(xT_kept, B)
            load_x(0, 0)
            load_x(1, 0)
            for u in range(2):
                for n in range(2):
                    parts_to_dram(n, False, u)
                for n in range(2):
                    parts_to_dram(n, True, u)
                if u == 0:
                    before_slots(0)
                    for n in (1, 0):
                        slots_from_dram(n, 0, slice(None))
                    sp.wait_ge(slots_in, SLOTS_IN)
            send_max(0, 0, 0)

            def row(jo, b, p):
                u = 2 * b + (2 * B * jo + p)
                first, last = (isinstance(b, int) and b == n for n in (0, B - 1))
                if first and p == 1 and jo > 0:
                    sp.wait_ge(wo_in, 32 * (jo + 1))
                one_more = not (last and p == 1 and jo + 1 == NJ)
                two_more = not (last and jo + 1 == NJ)
                if one_more:
                    before_slots(u + 1)
                    slots_from_dram(1, 1 - p, slice(0, 1))
                send_max(p, 1, u)
                if one_more:
                    slots_from_dram(1, 1 - p, slice(1, None))
                    slots_from_dram(0, 1 - p, slice(None))
                send_max(p, 2, u)
                if two_more:
                    load_x(p, 0 if last else b + 1)
                if last and jo + 1 < NJ:
                    load_v(p, jo + 1)
                if jo + 1 < NJ and (isinstance(b, int) and (b, p) in ((B - 2, 1), (B - 1, 0))):
                    load_qk(1 - p, jo + 1)
                if two_more:
                    sp.wait_ge(slots_in, SLOTS_IN * u + 2 * SLOTS_IN)
                    parts_to_dram(0, False, u + 2)
                    parts_to_dram(0, True, u + 2)
                    parts_to_dram(1, False, u + 2)
                send_max(p, 3, u)
                if two_more:
                    parts_to_dram(1, True, u + 2)
                if one_more:
                    send_max(1 - p, 0, u + 1)
                if last and p == 1 and jo + 1 < NJ:
                    emptied(sp, "o", 0, u - 1)
                    load_o(0, jo + 1)
                if first and p == 0 and jo > 0:
                    emptied(sp, "o", 0, u - 1)
                    load_o(1, jo)

            for jo in range(NJ):
                for p in range(2):
                    row(jo, 0, p)
                with sp.Fori(1, B - 2) as b:
                    for p in range(2):
                        row(jo, b, p)
                for b in (B - 2, B - 1):
                    for p in range(2):
                        row(jo, b, p)
            emptied(sp, "o", 0, UNITS - 1)
            sp.dma_start(out.rearrange("b (t p) e -> p (b t) e", p=P), acc[:]).then_inc(stored, 16)
            sp.wait_ge(stored, 16)
            for p in range(2):
                sp.wait_ge(xs_in[p], 8 * UNITS)
            sp.wait_ge(mrow_in, 16 * NG * UNITS)
            sp.wait_ge(parts_out, 64 * UNITS)
            sp.wait_ge(slots_in, SLOTS_IN * UNITS)

        @block.gpsimd
        def _(pool):
            own = Step(pool, pool_step)
            own.begin(0, 3)
            own(pool.memset(ident[:], 0.0))
            own(pool.affine_select(out=ident[:], in_=ident[:], compare_op=ALU.not_equal, fill=1.0, base=0,
                                   pattern=[[-1, P]], channel_multiplier=1))
            pool.tensor_copy(ident_bf[:], ident[:]).then_inc(ident_made, 1)
            pool.iota(idx[:], pattern=[[1, L]], base=0, channel_multiplier=0,
                      allow_small_or_imprecise_dtypes=True).then_inc(iota_made, 1)
            pool.iota(rank[:], pattern=[[-1, NE]], base=NE, channel_multiplier=0,
                      allow_small_or_imprecise_dtypes=True).then_inc(iota_made, 1)
            for p in range(2):
                pool.memset(vaug[p][:, :, :, D:V1], 1.0)
            own(pool.memset(mhalf[:], -0.5))
            own.end(1)
            with pool.Fori(0, B // 2) as i:
                for n in range(3):
                    for q in range(2):
                        pool.wait_ge(var_made, 6 * i + (2 * n + q + 1))
                        pool.tensor_tensor(rstd[q][:], veps[q][:], mhalf[:], ALU.pow).then_inc(rstd_made, 1)

            def unit(u):
                for n in range(2):
                    pool.wait_ge(hi_made, 2 * u + n + 1)
                    pool.tensor_tensor(rest[n][:], x32[n][:], parts[n][:, 0], ALU.subtract).then_inc(rest_made, 1)
                    pool.wait_ge(mid_made, 2 * u + n + 1)
                    pool.tensor_tensor(parts[n][:, 2], rest[n][:], parts[n][:, 1],
                                       ALU.subtract).then_inc(split_made, 1)

            for u in range(2):
                unit(u)
            with pool.Fori(2, UNITS) as u:
                unit(u)

        @block.tensor
        def _(pe):
            pe.wait_ge(ident_made, 1)
            pe.wait_ge(const_in, 16 * 11)
            half = B * L // 2
            for m in range(KT):
                for c in range(2):
                    for k in range(KT):
                        mm = pe.matmul(psS[0][:, 0:half] if (m, c) == (0, 0) else
                                       [psS[1], psS[2], psT[0]][2 * m + c - 1][:, 0:half],
                                       wa[:, k, m * P:m * P + P], encT[:, k, c * half:c * half + half],
                                       start=(k == 0), stop=(k == KT - 1))
                    mm.then_inc(waenc_ps, 1)
            pe.wait_ge(waenc_made, 4)

            def turn(q):
                for k in range(KT):
                    for t in range(TT):
                        mm = pe.transpose(bank_a[q][:, k * S + t * P:k * S + t * P + P],
                                          hn[q][:, t, k * P:k * P + P], ident[:])
                mm.then_inc(hnT_ps, 1)

            with pe.Fori(0, B // 2) as i:
                for q in range(2):
                    pe.wait_ge(hn_made, 4 * i + (q + 1))
                    turn(q)
                for q in range(2):
                    pe.wait_ge(hnT_made, 4 * i + (q + 1))
                    for t in range(TT):
                        for k in range(KT):
                            mm = pe.matmul(bank_b[q][:, t * L:t * L + L], hnT[q][:, k, t * P:t * P + P],
                                           waenc[:, k, bass.ds((2 * i + q) * L, L)],
                                           start=(k == 0), stop=(k == KT - 1))
                    mm.then_inc(score_ps, 1)
                for q in range(2):
                    pe.wait_ge(al_made, 2 * i + (q + 1))
                    for t in range(TT):
                        mm = pe.transpose(bank_b[q][0:L, S + t * P:S + t * P + P], al[q][:, t, :], ident[:])
                    mm.then_inc(alT_ps, 1)
                for q in range(2):
                    pe.wait_ge(alT_made, 2 * i + (q + 1))
                    pe.wait_ge(enc_in[q], 16 * i + 16)
                    for k in range(KT):
                        mm = pe.matmul(bank_c[q][:, k * S:k * S + S], enc[q][:, k * P:k * P + P], alT[q][:],
                                       start=True, stop=True)
                    mm.then_inc(cx_ps, 1)
                for q in range(2):
                    pe.wait_ge(cx_made, 2 * i + (q + 1))
                    for t in range(TT):
                        for k in range(2 * KT):
                            src = cxT[q] if k < KT else hnT[q]
                            mm = pe.matmul(bank_d[q][:, t * E:t * E + E], src[:, k % KT, t * P:t * P + P],
                                           wc[:, k, :], start=(k == 0), stop=(k == 2 * KT - 1))
                    mm.then_inc(co_ps, 1)
                for q in range(2):
                    pe.wait_ge(hn_made, 4 * i + (q + 3))
                    turn(q)
                for q in range(2):
                    pe.wait_ge(hnT_made, 4 * i + (q + 3))
                    for t in range(TT):
                        for k in range(KT):
                            mm = pe.matmul(bank_b[q][:, t * R:t * R + R], hnT[q][:, k, t * P:t * P + P], rw1[:, k, :],
                                           start=(k == 0), stop=(k == KT - 1))
                    mm.then_inc(rh_ps, 1)
                for q in range(2):
                    pe.wait_ge(rh_made, 2 * i + (q + 1))
                    for t in range(TT):
                        mm = pe.transpose(bank_b[q][:, S + t * P:S + t * P + P], rh[q][:, t, :], ident[:])
                    mm.then_inc(rhT_ps, 1)
                for q in range(2):
                    pe.wait_ge(rhT_made, 2 * i + (q + 1))
                    for t in range(TT):
                        mm = pe.matmul(bank_c[q][:, t * NE:t * NE + NE], rhT[q][:, t * P:t * P + P], rw2[:],
                                       start=True, stop=True)
                    mm.then_inc(lg_ps, 1)

            pe.wait_ge(gt_made, 1)
            banks = [psS[0], psS[1], psS[2], psT[0]]
            for t in range(NT):
                mm = pe.transpose(banks[t // 4][0:NE, (t % 4) * P:(t % 4) * P + P], gt[:, t, :], ident[:])
            mm.then_inc(gT_ps, 1)
            pe.wait_ge(gT_made, 1)
            for b in range(B):
                if b > 1:
                    pe.wait_ge(ob_added, b - 1)
                for t in range(TT):
                    mm = pe.matmul(psM[b % 2][:, t * E:t * E + E], gT[:, TT * b + t, :], obr[:],
                                   start=True, stop=True)
                mm.then_inc(ob_ps, 1)
            pe.wait_ge(ob_added, B)

            def project(what, n, p, u):
                ps, written = open_bank(pe, what, 0, u)
                for m in range(2):
                    for k in range(KT):
                        c = slice(m * P, m * P + P)
                        mm = (pe.matmul(ps[:, m * S:m * S + S], wqkv[p][:, n, k, c], xT[:, u % (2 * B) // 2, k, :],
                                        start=(k == 0), stop=(k == KT - 1)) if n < 2 else
                              pe.matmul(ps[:, m * E:m * E + E], xs[p][:, k, c], wqkv[p][:, n, k, :],
                                        start=(k == 0), stop=(k == KT - 1)))
                mm.then_inc(written, 1)

            def turn_max(g, u):
                pe.wait_ge(mhl_made, 4 * u + g + 1)
                ps, written = open_bank(pe, "m", g, u)
                for t in range(TT):
                    mm = pe.transpose(ps[:].bitcast(BF16)[0:2 * G, t * P:t * P + P], mhl[g % 2][:, t, :], ident_bf[:])
                mm.then_inc(written, 1)

            def scores(p, g, j, u):
                h = G * g + j
                if h == 0:
                    pe.wait_ge(slots_in, SLOTS_IN * u + SLOTS_IN)
                n = H * u + h
                if not (isinstance(n, int) and n < BACK[j]):
                    pe.wait_ge(max_made, n - BACK[j] + 1)
                for t in range(TT):
                    mm = pe.matmul(psS[S_BANK[j]][:, t * S:t * S + S], Qp[p][0:KR, h, t * P:t * P + P],
                                   Kp[p][0:KR, h, :], start=True, stop=True)
                mm.then_inc(s_ps, 1)

            def scores_T(p, h, u):
                n = H * u + h
                if not (isinstance(n, int) and n < 2):
                    pe.wait_ge(exp_made, n - 1)
                for k in range(TT):
                    mm = pe.matmul(psT[h % 2][:, k * S:k * S + S], Kp[p][0:KM, h, k * P:k * P + P],
                                   Qp[p][0:KM, h, :], start=True, stop=True)
                mm.then_inc(t_ps, 1)

            def values(p, h, u):
                g, j = h // G, h % G
                if h == 0:
                    emptied(pe, "v", 0, u)
                if j == 0 and not (isinstance(u, int) and NG * u + g == 0):
                    pe.wait_ge(oun_made, NG * u + g)
                pe.wait_ge(exp_made, H * u + h + 1)
                for k in range(TT):
                    mm = pe.matmul(psV[32 * j:32 * j + V1, (g % 2) * S:(g % 2) * S + S],
                                   vaug[p][:, k, h, :], pexp[h % NP_][:, k, :],
                                   start=(k == 0), stop=(k == TT - 1))
                if j == G - 1:
                    mm.then_inc(pv_ps, 1)

            def by_token(t, u):
                pe.wait_ge(oun_made, NG * u + NG)
                ps, written = open_bank(pe, "t1", t, u)
                for g in range(NG):
                    mm = pe.transpose(ps[:, g * P:g * P + P], oun[:, g, t * P:t * P + P], ident[:])
                mm.then_inc(written, 1)

            def by_width(u):
                for t in range(TT):
                    emptied(pe, "t1", t, u)
                ps, written = open_bank(pe, "t2", 0, u)
                for k in range(KT):
                    for t in range(TT):
                        mm = pe.transpose(ps[:, k * S + t * P:k * S + t * P + P],
                                          onm[:, t, k * H // KT:(k + 1) * H // KT, :].rearrange("p h d -> p (h d)"),
                                          ident[:])
                mm.then_inc(written, 1)

            def output(p, u):
                emptied(pe, "t2", 0, u)
                ps, written = open_bank(pe, "o", 0, u)
                for t in range(TT):
                    for k in range(KT):
                        mm = pe.matmul(ps[:, t * E:t * E + E], onT[:, k, t * P:t * P + P], wo[p][:, k, :],
                                       start=(k == 0), stop=(k == KT - 1))
                mm.then_inc(written, 1)

            def extra(what, g, p, u):
                if what == "m":
                    turn_max(g, u)
                elif what == "t1":
                    by_token(g, u)
                elif what == "t2":
                    by_width(u)
                elif what == "o":
                    output(p, u)
                else:
                    if what == "pq":
                        pe.wait_ge(wqk_in[p], 32 * (u // (2 * B)) + 32)
                    elif what == "v":
                        pe.wait_ge(wv_in[p], 32 * (u // (2 * B)) + 32)
                        pe.wait_ge(xs_in[p], 8 * (u - p) + 16)
                    project(what, {"pq": 0, "pk": 1, "v": 2}[what], p, u)

            extra("pq", 0, 0, 0)
            extra("pk", 0, 0, 0)
            extra("v", 0, 0, 0)
            extra("pq", 0, 1, 1)
            extra("pk", 0, 1, 1)
            for j in range(G):
                scores(0, 0, j, 0)
            turn_max(0, 0)
            for j in range(G):
                scores(0, 1, j, 0)

            def quarter(u, g, p):
                sg, du = S_AHEAD[g]
                pe.wait_ge(mrow_in, 16 * NG * u + 16 * (g + 1))
                for j in range(G):
                    if there(u + du):
                        scores((p + du) % 2, sg, j, u + du)
                    h = G * g + j
                    scores_T(p, h, u)
                    if j != 2:
                        if h >= 2:
                            values(p, h - 2, u)
                        elif there(u - 1):
                            values(1 - p, H + h - 2, u - 1)
                    for what, eg, _ in EXTRAS[g][j]:
                        v = unit_of(what, eg, u)
                        if there(v):
                            extra(what, eg, (p + unit_of(what, eg, 0)) % 2, v)
                    if j == 2:
                        values(p, h - 2, u)

            rows(pe, quarter)
            values(1, H - 2, UNITS - 1)
            values(1, H - 1, UNITS - 1)
            for what, eg in (("t1", 0), ("t1", 1), ("t2", 0), ("o", 0)):
                extra(what, eg, 1, UNITS - 1)

        @block.scalar
        def _(act):
            act.wait_ge(gauss_arg, 1)
            act.activation(gauss[:], gauss[:], ACT.Exp, scale=-1.0 / DEV_POW).then_inc(gauss_made, 1)
            half = B * L // 2
            for n in range(4):
                act.wait_ge(waenc_ps, n + 1)
                src = [psS[0], psS[1], psS[2], psT[0]][n]
                act.activation(waenc[:, n // 2, (n % 2) * half:(n % 2) * half + half], src[:, 0:half],
                               ACT.Copy).then_inc(waenc_made, 1)
            def flat(a):
                return a[:].rearrange("p k s -> p (k s)")

            with act.Fori(0, B // 2) as i:
                for q in range(2):
                    act.wait_ge(hnT_ps, 4 * i + (q + 1))
                    act.activation(flat(hnT[q]), bank_a[q][:], ACT.Copy).then_inc(hnT_made, 1)
                for q in range(2):
                    act.wait_ge(smax_made, 2 * i + (q + 1))
                    for t in range(TT):
                        act.activation(sc[q][:, t, :], sc[q][:, t, :], ACT.Exp, bias=smx[q][:, t:t + 1],
                                       accum_out=ssum[q][:, t:t + 1]).then_inc(sexp_made, 1)
                for q in range(2):
                    act.wait_ge(alT_ps, 2 * i + (q + 1))
                    act.activation(alT[q][:], bank_b[q][0:L, S:2 * S], ACT.Copy).then_inc(alT_made, 1)
                for q in range(2):
                    act.wait_ge(cx_ps, 2 * i + (q + 1))
                    act.activation(flat(cxT[q]), bank_c[q][:], ACT.Copy).then_inc(cx_made, 1)
                for q in range(2):
                    act.wait_ge(co_ps, 2 * i + (q + 1))
                    act.activation(flat(th[q]), bank_d[q][:], ACT.Tanh).then_inc(tanh_made, 1)
                for q in range(2):
                    act.wait_ge(hnT_ps, 4 * i + (q + 3))
                    act.activation(flat(hnT[q]), bank_a[q][:], ACT.Copy).then_inc(hnT_made, 1)
                for q in range(2):
                    act.activation(xT[:, 2 * i + q].rearrange("p k s -> p (k s)"), bank_a[q][:],
                                   ACT.Copy).then_inc(xT_kept, 1)
                for q in range(2):
                    act.wait_ge(rhT_ps, 2 * i + (q + 1))
                    act.activation(rhT[q][:], bank_b[q][:, S:2 * S], ACT.Copy).then_inc(rhT_made, 1)
            act.wait_ge(lsub_made, 1)
            act.activation(pr[:], lg[:], ACT.Exp).then_inc(lexp_made, 1)
            act.wait_ge(gT_ps, 1)
            for n in range(4):
                last = act.activation(gT[:, 4 * n:4 * n + 4, :].rearrange("p a b -> p (a b)"),
                                      [psS[0], psS[1], psS[2], psT[0]][n][0:NE, :], ACT.Copy)
            last.then_inc(gT_made, 1)

            def keep_max(g, u):
                ps, free = bank_written(act, "m", g, u)
                act.activation(mT[g % 2][:], ps[:].bitcast(BF16)[0:2 * G, 0:S], ACT.Copy).then_inc(free, 1)

            def middle(n, u):
                act.wait_ge(rest_made, 2 * u + n + 1)
                act.activation(parts[n][:, 1], rest[n][:], ACT.Copy).then_inc(mid_made, 1)

            for u in range(2):
                middle(0, u)
                middle(1, u)
            keep_max(0, 0)

            def undivided(g, u):
                act.wait_ge(pv_ps, NG * u + g + 1)
                act.activation(oun[:, g, :], psV[:, (g % 2) * S:(g % 2) * S + S], ACT.Copy).then_inc(oun_made, 1)

            def keep_on(u):
                ps, free = bank_written(act, "t2", 0, u)
                act.activation(onT[:].rearrange("p k s -> p (k s)"), ps[:], ACT.Copy).then_inc(free, 1)

            def quarter(u, g, p):
                for j in range(G):
                    h = G * g + j
                    act.wait_ge(t_ps, H * u + h + 1)
                    act.activation(pexp[h % NP_][:].rearrange("p k s -> p (k s)"), psT[h % 2][:],
                                   ACT.Exp, scale=SCALE).then_inc(exp_made, 1)
                    if j == 1:
                        if g > 0:
                            undivided(g - 1, u)
                        elif there(u - 1):
                            undivided(NG - 1, u - 1)
                    if there(u + 2) and (g, j) in MIDDLE:
                        middle(MIDDLE.index((g, j)), u + 2)
                    for what, eg, _ in EXTRAS[g][j]:
                        v = unit_of(what, eg, u)
                        if there(v):
                            if what == "m":
                                keep_max(eg, v)
                            elif what == "t2":
                                keep_on(v)

            rows(act, quarter)
            undivided(NG - 1, UNITS - 1)
            keep_on(UNITS - 1)

        @block.vector
        def _(dve):
            own = Step(dve, dve_step)
            own.begin(0, 8)
            dve.memset(psV[:], 0.0)
            for p in range(2):
                dve.memset(Kp[p][KR:KM], 1.0)
            dve.wait_ge(iota_made, 2)
            dve.wait_ge(bc_in, 32)
            own(dve.tensor_scalar(w_start[:], pt[:], -WINDOW, 0.0, ALU.add, ALU.max))
            own(dve.tensor_scalar(w_end[:], pt[:], WINDOW, None, ALU.add))
            own(dve.tensor_copy(len_f[:], len_i[:]))
            own(dve.tensor_tensor(w_end[:], w_end[:], len_f[:], ALU.min))
            idx_b = idx[:].unsqueeze(1).to_broadcast([P, B, L])

            def per_batch(a):
                return a[:].unsqueeze(2).to_broadcast([P, B, L])

            own(dve.tensor_tensor(keep[:], idx_b, per_batch(w_start), ALU.is_ge))
            own(dve.tensor_tensor(keep2[:], idx_b, per_batch(w_end), ALU.is_le))
            own(dve.tensor_tensor(keep[:], keep[:], keep2[:], ALU.mult))
            dve.tensor_scalar(fill[:], keep[:], NEG, -NEG, ALU.mult, ALU.add)
            own(dve.tensor_tensor(gauss[:], idx_b, per_batch(pt), ALU.subtract))
            dve.tensor_tensor(gauss[:], gauss[:], gauss[:], ALU.mult).then_inc(gauss_arg, 1)
            own.end(1)
            dve.wait_ge(gauss_made, 1)
            dve.wait_ge(x_in, 16)
            dve.wait_ge(const_in, 16 * 11)

            def stats_of(tiles, q):
                for t in range(TT):
                    last = dve.bn_stats(stats[q][:, t, :], tiles[t])
                own(last, apart)
                for t in range(TT):
                    last = dve.bn_aggr(mv[q][:, t, :], stats[q][:, t, :])
                own(last)
                dve.tensor_scalar(veps[q][:], mv[q][:, :, 1], EPS, None, ALU.add).then_inc(var_made, 1)

            def normalise(dst, tiles, n, i, q):
                dve.wait_ge(rstd_made, 6 * i + (2 * n + q + 1))
                for t in range(TT):
                    last = dve.tensor_scalar(dst[:, t, :], tiles[t], mv[q][:, t, 0:1], rstd[q][:, t:t + 1],
                                             ALU.subtract, ALU.mult)
                return last

            with dve.Fori(0, B // 2) as i:
                own.begin(i, 32)
                tiles = [[acc[:, TT * (2 * i + q) + t, :] for t in range(TT)] for q in range(2)]
                two = [acc[:, bass.ds(TT * (2 * i + q), TT), :] for q in range(2)]
                rtiles = [[rh[q][:, t, :] for t in range(TT)] for q in range(2)]
                for q in range(2):
                    stats_of(tiles[q], q)
                for q in range(2):
                    normalise(hn[q], tiles[q], 0, i, q).then_inc(hn_made, 1)
                for q in range(2):
                    dve.wait_ge(score_ps, 2 * i + (q + 1))
                    kb_ = keep[:, bass.ds(2 * i + q, 1), :].to_broadcast([P, TT, L])
                    fb_ = fill[:, bass.ds(2 * i + q, 1), :].to_broadcast([P, TT, L])
                    own(dve.tensor_tensor(sc[q][:], bank_b[q][:, 0:TT * L].rearrange("p (t l) -> p t l", t=TT), kb_,
                                          ALU.mult))
                    own(dve.tensor_tensor(sc[q][:], sc[q][:], fb_, ALU.add))
                    dve.tensor_reduce(smx[q][:], sc[q][:], AX.X, ALU.max, negate=True).then_inc(smax_made, 1)
                for q in range(2):
                    dve.wait_ge(sexp_made, 4 * i + (TT * q + TT))
                    own(dve.reciprocal(ssum[q][:], ssum[q][:]))
                    own(dve.tensor_tensor(sc[q][:], sc[q][:], ssum[q][:].unsqueeze(2).to_broadcast([P, TT, L]),
                                          ALU.mult))
                    dve.tensor_tensor(al[q][:], sc[q][:], gauss[:, bass.ds(2 * i + q, 1), :].to_broadcast([P, TT, L]),
                                      ALU.mult).then_inc(al_made, 1)
                for q in range(2):
                    dve.wait_ge(tanh_made, 2 * i + (q + 1))
                    own(dve.tensor_tensor(two[q], two[q], th[q][:], ALU.add), apart)
                    stats_of(tiles[q], q)
                for q in range(2):
                    normalise(hn[q], tiles[q], 1, i, q).then_inc(hn_made, 1)
                for q in range(2):
                    dve.wait_ge(rh_ps, 2 * i + (q + 1))
                    own(dve.tensor_tensor(rh[q][:], bank_b[q][:, 0:TT * R].rearrange("p (t r) -> p t r", t=TT),
                                          rb1_b[:].unsqueeze(1).to_broadcast([P, TT, R]), ALU.add))
                    stats_of(rtiles[q], q)
                for q in range(2):
                    own(normalise(rh[q], rtiles[q], 2, i, q))
                    own(dve.tensor_tensor(rh[q][:], rh[q][:], lng_b[:].unsqueeze(1).to_broadcast([P, TT, R]),
                                          ALU.mult))
                    own(dve.tensor_tensor(rh[q][:], rh[q][:], lnb_b[:].unsqueeze(1).to_broadcast([P, TT, R]), ALU.add))
                    dve.tensor_scalar(rh[q][:], rh[q][:], 0.0, None, ALU.max).then_inc(rh_made, 1)
                for q in range(2):
                    dve.wait_ge(lg_ps, 2 * i + (q + 1))
                    own(dve.tensor_tensor(lg[:, bass.ds(TT * (2 * i + q), TT), :],
                                          bank_c[q][:, 0:TT * NE].rearrange("p (t e) -> p t e", t=TT),
                                          rb2_b[:].unsqueeze(1).to_broadcast([P, TT, NE]), ALU.add))
            own.end(B // 2)

            def per_token(a):
                return a[:].unsqueeze(2).to_broadcast([P, NT, NE])

            rank_b = rank[:].unsqueeze(1).to_broadcast([P, NT, NE])
            own.begin(0, 18)
            own(dve.tensor_reduce(r1[:], lg[:], AX.X, ALU.max))
            dve.tensor_tensor(lg[:], lg[:], per_token(r1), ALU.subtract).then_inc(lsub_made, 1)
            dve.wait_ge(lexp_made, 1)
            own(dve.reduce_sum(r2[:], pr[:], AX.X))
            own(dve.reciprocal(r2[:], r2[:]))
            own(dve.tensor_tensor(pr[:], pr[:], per_token(r2), ALU.mult))

            def pick(src, top, one_hot):
                own(dve.tensor_reduce(top[:], src[:], AX.X, ALU.max))
                own(dve.tensor_tensor(eq[:], src[:], per_token(top), ALU.is_equal))
                own(dve.tensor_tensor(eq[:], eq[:], rank_b, ALU.mult))
                own(dve.tensor_reduce(r3[:], eq[:], AX.X, ALU.max))
                own(dve.tensor_tensor(one_hot[:], eq[:], per_token(r3), ALU.is_equal))

            pick(pr, r1, oh1)
            own(dve.scalar_tensor_tensor(pr2[:].rearrange("p a b -> p (a b)"), oh1[:].rearrange("p a b -> p (a b)"),
                                         -2.0, pr[:].rearrange("p a b -> p (a b)"), ALU.mult, ALU.add))
            pick(pr2, r2, oh2)
            own(dve.tensor_tensor(r1[:], r1[:], r2[:], ALU.add))
            own(dve.reciprocal(r1[:], r1[:]))
            own(dve.tensor_tensor(oh1[:], oh1[:], oh2[:], ALU.add))
            own.end(1)
            own.begin(0, 2)
            own(dve.tensor_tensor(oh1[:], oh1[:], pr[:], ALU.mult))
            dve.tensor_tensor(gt[:], oh1[:], per_token(r1), ALU.mult).then_inc(gt_made, 1)
            dve.wait_ge(gt_made, 1)
            for q in range(2):
                last = dve.tensor_copy(
                    gates[:].rearrange("p (j b q t) -> p q j b t", j=NJ, b=B, q=2)[:, q],
                    gt[:].rearrange("p (b t) (j q) -> p q j b t", b=B, j=NJ)[:, q])
            own(last)
            own.end(1)
            for b in range(B):
                dve.wait_ge(ob_ps, b + 1)
                a = acc[:, TT * b:TT * b + TT, :]
                dve.tensor_tensor(a, a, psM[b % 2][:].rearrange("p (t e) -> p t e", t=TT),
                                  ALU.add).then_inc(ob_added, 1)

            def keep_32(what, n, u):
                ps, free = bank_written(dve, what, 0, u)
                if not (isinstance(u, int) and u == 0):
                    dve.wait_ge(split_made, 2 * u)
                    dve.wait_ge(parts_out, 64 * u)
                e = 2 * (u // (2 * B)) + u % 2
                dve.tensor_tensor(x32[n][:], ps[:].rearrange("p (k s) -> p k s", k=KT),
                                  bqk[:, bass.ds(NE * n + e, 1), :].rearrange("p o k -> p k o")
                                  .to_broadcast([P, KT, S]), ALU.add).then_inc(free, 1)
                emptied(dve, what, 0, u)
                dve.tensor_copy(parts[n][:, 0], x32[n][:]).then_inc(hi_made, 1)

            def keep_v(p, u):
                ps, free = bank_written(dve, "v", 0, u)
                dve.tensor_tensor(vaug[p][:, :, :, 0:D], ps[:].rearrange("p (t h d) -> p t h d", t=TT, h=H),
                                  bv[p][:].rearrange("p (h d) -> p h d", h=H).unsqueeze(1)
                                  .to_broadcast([P, TT, H, D]), ALU.add).then_inc(free, 1)

            def head_max(g, j, u):
                dve.wait_ge(s_ps, 16 * u + G * g + j + 1)
                dve.tensor_reduce(negm[g % 2][:, :, j], psS[S_BANK[j]][:].rearrange("p (t s) -> p t s", t=TT), AX.X,
                                  ALU.max, negate=True).then_inc(max_made, 1)

            def split_max(g, u):
                dve.wait_ge(max_made, 16 * u + G * g + G)
                dve.tensor_copy(mhl[g % 2][:, :, 0:G], negm[g % 2][:]).then_inc(mhi_made, 1)
                dve.wait_ge(mhi_made, 4 * u + g + 1)
                dve.tensor_tensor(mhl[g % 2][:, :, G:2 * G], negm[g % 2][:], mhl[g % 2][:, :, 0:G],
                                  ALU.subtract).then_inc(mhl_made, 1)

            keep_32("pq", 0, 0)
            keep_32("pk", 1, 0)
            keep_v(0, 0)
            keep_32("pq", 0, 1)
            keep_32("pk", 1, 1)
            for g in range(2):
                for j in range(G):
                    head_max(g, j, 0)
                split_max(g, 0)

            def divide(t, u):
                ps, free = bank_written(dve, "t1", t, u)
                heads = ps[:].rearrange("p (h c) -> p h c", h=H)
                dve.reciprocal(rcp[:, t, :], heads[:, :, D]).then_inc(rcp_made, 1)
                dve.wait_ge(rcp_made, 2 * u + t + 1)
                dve.tensor_scalar(rgt[:, t, :], rcp[:, t, :], gates[:, bass.ds(TT * u + t, 1)], None,
                                  ALU.mult).then_inc(rgt_made, 1)
                dve.wait_ge(rgt_made, 2 * u + t + 1)
                dve.tensor_tensor(onm[:, t], heads[:, :, 0:D],
                                  rgt[:, t, :].unsqueeze(2).to_broadcast([P, H, D]), ALU.mult).then_inc(free, 1)

            def accumulate(b, u):
                ps, free = bank_written(dve, "o", 0, u)
                a = acc[:, bass.ds(TT * b, TT), :]
                dve.tensor_tensor(a, a, ps[:].rearrange("p (t e) -> p t e", t=TT), ALU.add).then_inc(free, 1)

            def quarter(u, g, p):
                sg, du = S_AHEAD[g]
                for j in range(G):
                    if there(u + du):
                        head_max(sg, j, u + du)
                    if j == G - 1 and there(u + du):
                        split_max(sg, u + du)
                    for what, eg, _ in EXTRAS[g][j]:
                        v = unit_of(what, eg, u)
                        if there(v):
                            vp = (p + unit_of(what, eg, 0)) % 2
                            if what == "t1":
                                divide(eg, v)
                            elif what == "o":
                                accumulate((v - vp) % (2 * B) // 2, v)
                            elif what == "v":
                                keep_v(vp, v)
                            elif what == "pq":
                                keep_32("pq", 0, v)
                            elif what == "pk":
                                keep_32("pk", 1, v)

            rows(dve, quarter)
            divide(0, UNITS - 1)
            divide(1, UNITS - 1)
            accumulate(B - 1, UNITS - 1)


def kernel(**inputs):
    import numpy as np
    import concourse.bacc as bacc
    from concourse.bass_utils import run_bass_kernel_spmd

    def turned(a):
        return np.ascontiguousarray(np.swapaxes(a, -1, -2))

    def by_row(w):
        n, e_out, e_in = w.shape
        return np.ascontiguousarray(w.reshape(n, hp, kt, d, e_in).transpose(0, 4, 2, 3, 1).reshape(n, e_in, e_out))

    heads, kt = 16, 2
    i = {k: np.asarray(v) for k, v in inputs.items()}
    f = {n: i["L0_ffn_" + n] for n in ("rW1", "rb1", "ln_g", "ln_b", "rW2", "rb2", "qW", "qb", "kW", "kb",
                                       "vW", "vb", "oW", "ob")}
    ctx = i["ctx_1024"]
    d = f["qW"].shape[1] // heads
    hp = heads // kt
    arrays = {
        "x": i["x"], "ctx_e": ctx,
        "ctx_t": np.ascontiguousarray(ctx.transpose(2, 0, 1).reshape(ctx.shape[2], -1)),
        "p_t": i["condB_pt"], "src_len": i["_lenS2"],
        "waT": turned(i["L0_xcond_W_a"]), "wcT": turned(i["L0_xcond_W_c"]),
        "rw1T": turned(f["rW1"]), "rb1": f["rb1"], "ln_g": f["ln_g"], "ln_b": f["ln_b"],
        "rw2T": turned(f["rW2"]), "rb2": f["rb2"],
        "qwT": by_row(f["qW"]), "kwT": by_row(f["kW"]),
        "qkb": np.ascontiguousarray(np.stack([f["qb"], f["kb"]]).reshape(-1, hp, kt, d)
                                    .transpose(3, 1, 0, 2).reshape(128, -1, kt)),
        "vwT": turned(f["vW"]), "vb": f["vb"], "owT": turned(f["oW"]), "ob": f["ob"],
    }
    nc = bacc.Bacc("TRN2", target_bir_lowering=False, num_devices=1)
    args = {n: nc.dram_tensor("in_" + n, a.shape, mybir.dt.from_np(a.dtype), kind="ExternalInput").ap()
            for n, a in arrays.items()}
    out = nc.dram_tensor("out_0", i["x"].shape, F32, kind="ExternalOutput").ap()
    pixart_block(nc, out=out, **args)
    r = run_bass_kernel_spmd(nc, [{"in_" + n: np.ascontiguousarray(a) for n, a in arrays.items()}], core_ids=[0])
    return r.results[0]["out_0"]
```

```python
from contextlib import ExitStack

import concourse.bass as bass
from concourse import mybir

ALU = mybir.AluOpType
ACT = mybir.ActivationFunctionType
AX = mybir.AxisListType
F32 = mybir.dt.float32
BF16 = mybir.dt.bfloat16
I32 = mybir.dt.int32


class Step:

    def __init__(self, eng, sem):
        self.eng, self.sem, self.done = eng, sem, 0

    def begin(self, turn, per):
        self.turn, self.per, self.local = turn, per, 0

    def __call__(self, ins, apart=None):
        self.local += 1
        ins.then_inc(self.sem, 1)
        self.eng.wait_ge(self.sem, self.turn * self.per + (self.done + self.local))
        if apart:
            apart(self.eng)

    def end(self, turns):
        assert self.local == self.per, self.local
        self.done += turns * self.per


def pixart_block(nc, x, ctx_e, ctx_t, p_t, src_len, waT, wcT, rw1T, rb1, ln_g, ln_b, rw2T, rb2,
                 qwT, kwT, qkb, vwT, vb, owT, ob, out):
    B, S, E = x.shape
    L = ctx_e.shape[1]
    NE = qwT.shape[0]
    R = rw1T.shape[1]
    H = 16
    D = E // H
    P = 128
    TT = S // P
    KT = E // P
    NT = B * TT
    G = 4
    NG = H // G
    V1 = D + 1
    KR = 6 * D
    KM = KR + 2
    SCALE = float(D) ** -0.5
    WINDOW, DEV_POW, NEG, EPS = 16.0, 128.0, 1e9, 1e-5
    assert TT == 2 and KT == 2 and NG == 4 and E == H * D and NE % 2 == 0 and R == P
    NJ = NE // 2
    HP = P // D
    PARTS = (((0, 1), 0), ((0, 1), 2), ((0,), 4), ((2,), 5)), (((0, 1, 2), 0), ((0, 1), 3), ((0,), 5))
    order = [[m for run, _ in PARTS[n] for m in run] for n in range(2)]
    assert sorted(zip(*order)) == [(0, 0), (0, 1), (0, 2), (1, 0), (1, 1), (2, 0)]

    with ExitStack() as st:
        def sb(name, shape, dt=F32):
            return st.enter_context(nc.sbuf_tensor(name, shape, dt))

        def psum(name):
            return st.enter_context(nc.psum_tensor(name, [P, 512], F32))

        def sem(name):
            return st.enter_context(nc.semaphore(name))

        acc = sb("acc", [P, NT, E])
        xT = sb("xT", [P, B, KT, S])
        gates = sb("gates", [P, NE * NT])
        ident = sb("ident", [P, P])
        ident_bf = sb("ident_bf", [P, P], BF16)
        enc = [sb(f"enc{q}", [L, E]) for q in range(2)]
        encT = sb("encT", [P, KT, B * L])
        wa = sb("wa", [P, KT, E])
        wc = sb("wc", [P, 2 * KT, E])
        waenc = sb("waenc", [P, KT, B * L])
        pt = sb("pt", [P, B])
        len_i = sb("len_i", [P, B], I32)
        len_f = sb("len_f", [P, B])
        w_start = sb("w_start", [P, B])
        w_end = sb("w_end", [P, B])
        idx = sb("idx", [P, L])
        keep = sb("keep", [P, B, L])
        keep2 = sb("keep2", [P, B, L])
        fill = sb("fill", [P, B, L])
        gauss = sb("gauss", [P, B, L])
        rw1 = sb("rw1", [P, KT, R])
        rw2 = sb("rw2", [R, NE])
        rb1_b = sb("rb1_b", [P, R])
        lng_b = sb("lng_b", [P, R])
        lnb_b = sb("lnb_b", [P, R])
        rb2_b = sb("rb2_b", [P, NE])
        obr = sb("obr", [NE, E])
        mhalf = sb("mhalf", [P, TT])
        carry = sb("carry", [P, 8])
        stats = [sb(f"stats{q}", [P, TT, 6]) for q in range(2)]
        mv = [sb(f"mv{q}", [P, TT, 2]) for q in range(2)]
        veps = [sb(f"veps{q}", [P, TT]) for q in range(2)]
        rstd = [sb(f"rstd{q}", [P, TT]) for q in range(2)]
        hn1 = [sb(f"hn1_{q}", [P, TT, E]) for q in range(2)]
        hn2 = [sb(f"hn2_{q}", [P, TT, E]) for q in range(2)]
        hn1T = [sb(f"hn1T_{q}", [P, KT, S]) for q in range(2)]
        hn2T = [sb(f"hn2T_{q}", [P, KT, S]) for q in range(2)]
        sc = [sb(f"sc{q}", [P, TT, L]) for q in range(2)]
        smx = [sb(f"smx{q}", [P, TT]) for q in range(2)]
        ssum = [sb(f"ssum{q}", [P, TT]) for q in range(2)]
        al = [sb(f"al{q}", [P, TT, L]) for q in range(2)]
        alT = [sb(f"alT{q}", [L, S]) for q in range(2)]
        cxT = [sb(f"cxT{q}", [P, KT, S]) for q in range(2)]
        th = [sb(f"th{q}", [P, TT, E]) for q in range(2)]
        rh = [sb(f"rh{q}", [P, TT, R]) for q in range(2)]
        rhT = [sb(f"rhT{q}", [P, S]) for q in range(2)]
        lg = sb("lg", [P, NT, NE])
        rank = sb("rank", [P, NE])
        pr = sb("pr", [P, NT, NE])
        pr2 = sb("pr2", [P, NT, NE])
        eq = sb("eq", [P, NT, NE])
        oh1 = sb("oh1", [P, NT, NE])
        oh2 = sb("oh2", [P, NT, NE])
        r1 = sb("r1", [P, NT])
        r2 = sb("r2", [P, NT])
        r3 = sb("r3", [P, NT])
        gt = sb("gt", [P, NT, NE])
        gT = sb("gT", [NE, NT, P])
        xs = [sb(f"xs{p}", [P, KT, S]) for p in range(2)]
        wqkv = [sb(f"wqkv{p}", [P, 3, KT, E]) for p in range(2)]
        bqk = sb("bqk", [P, 2 * NE, KT])
        bv = [sb(f"bv{p}", [P, E]) for p in range(2)]
        wo = [sb(f"wo{p}", [P, KT, E]) for p in range(2)]
        x32 = [sb(f"x32{n}", [P, KT, S]) for n in range(2)]
        rest = [sb(f"rest{n}", [P, KT, S]) for n in range(2)]
        parts = [sb(f"parts{n}", [P, 3, KT, S], BF16) for n in range(2)]
        packed = [nc.dram_tensor(f"packed{n}", (3, P, KT * S), BF16).ap() for n in range(2)]
        Qp = [sb(f"Qp{p}", [KM, H, S], BF16) for p in range(2)]
        Kp = [sb(f"Kp{p}", [KM, H, S], BF16) for p in range(2)]
        vaug = [sb(f"vaug{p}", [P, TT, H, V1]) for p in range(2)]
        negm = [sb(f"negm{p}", [P, TT, G]) for p in range(2)]
        mhl = [sb(f"mhl{p}", [P, TT, 2 * G], BF16) for p in range(2)]
        mT = [sb(f"mT{p}", [2 * G, S], BF16) for p in range(2)]
        NP_ = 4
        pexp = [sb(f"pexp{n}", [P, TT, S]) for n in range(NP_)]
        oun = [sb(f"oun{p}", [P, NG, S]) for p in range(2)]
        rcp = sb("rcp", [P, TT, H])
        onm = sb("onm", [P, TT, H, D])
        onT = sb("onT", [P, KT, S])

        S_BANK, BACK = (0, 1, 2, 1), (4, 2, 4, 2)
        psS = [psum(f"psS{n}") for n in range(3)]
        psT = [psum(f"psT{n}") for n in range(2)]
        psV = psum("psV")
        psM = [psum("psA"), psum("psB")]
        bank_a, bank_b, bank_d, bank_r = (psS[0], psS[1]), (psS[2], psT[0]), (psM[0], psM[1]), (psT[1], psV)
        bank_ob = (psT[1], psV)

        x_in, wa_in, const_in, bc_in = sem("x_in"), sem("wa_in"), sem("const_in"), sem("bc_in")
        enc_in = [sem(f"enc_in{q}") for q in range(2)]
        wqk_in, wv_in = [sem(f"wqk_in{p}") for p in range(2)], [sem(f"wv_in{p}") for p in range(2)]
        wo_in, mrow_in, stored = sem("wo_in"), sem("mrow_in"), sem("stored")
        xs_in = [sem(f"xs_in{p}") for p in range(2)]
        ident_made, iota_made, pool_step = sem("ident_made"), sem("iota_made"), sem("pool_step")
        dve_step = sem("dve_step")
        gauss_arg, gauss_made = sem("gauss_arg"), sem("gauss_made")
        waenc_ps, waenc_made = sem("waenc_ps"), sem("waenc_made")
        var_made, rstd_made = sem("var_made"), sem("rstd_made")
        hn1_made, hn2_made, hn1T_ps, hn1T_made = (sem("hn1_made"), sem("hn2_made"),
                                                    sem("hn1T_ps"), sem("hn1T_made"))
        hn2T_ps, hn2T_made = sem("hn2T_ps"), sem("hn2T_made")
        score_ps, smax_made, sexp_made = sem("score_ps"), sem("smax_made"), sem("sexp_made")
        al_made, alT_ps, alT_made = sem("al_made"), sem("alT_ps"), sem("alT_made")
        cx_ps, cx_made, co_ps, tanh_made = sem("cx_ps"), sem("cx_made"), sem("co_ps"), sem("tanh_made")
        rh_ps, rh_made, rhT_ps, rhT_made, lg_ps = (sem("rh_ps"), sem("rh_made"), sem("rhT_ps"),
                                                   sem("rhT_made"), sem("lg_ps"))
        lsub_made, lexp_made, gt_made, gT_ps, gT_made, ob_ps, ob_added = (
            sem("lsub_made"), sem("lexp_made"), sem("gt_made"), sem("gT_ps"), sem("gT_made"),
            sem("ob_ps"), sem("ob_added"))
        s_ps, max_made, t_ps, exp_made = sem("s_ps"), sem("max_made"), sem("t_ps"), sem("exp_made")
        pv_ps, oun_made = sem("pv_ps"), sem("oun_made")
        misc_ps = [sem("miscA_ps"), sem("miscB_ps")]
        misc_free = [sem("miscA_free"), sem("miscB_free")]
        mhi_made, mhl_made = sem("mhi_made"), sem("mhl_made")
        rcp_made = sem("rcp_made")
        hi_made, mid_made, rest_made = sem("hi_made"), sem("mid_made"), sem("rest_made")
        split_made = sem("split_made")
        parts_out, slots_in = sem("parts_out"), sem("slots_in")

        EXTRAS = [[[], [("m", 1, 1)], [("pq", 0, 0)], [("t1", 0, 1)]],
                  [[("t1", 1, 0)], [("m", 2, 1)], [("pk", 0, 1)], [("t2", 0, 0)]],
                  [[], [("m", 3, 0)], [("o", 0, 1)], []],
                  [[], [("m", 0, 1), ("v", 0, 0)], [], []]]
        ROW = [e for quarter in EXTRAS for step in quarter for e in step]
        UNITS = NE * B

        def unit_of(what, g, row):
            return row + {"pq": 2, "pk": 2, "v": 1, "t1": -1, "t2": -1, "o": -1}.get(
                what, 1 if (what, g) == ("m", 0) else 0)

        BEFORE = [("pq", 0, 0), ("pk", 0, 0), ("v", 0, 0), ("pq", 0, 1), ("pk", 0, 1), ("m", 0, 0)]
        bank_of = {(w, g): b for w, g, b in ROW}
        per_row = [sum(b == n for _, _, b in ROW) for n in range(2)]
        ordinal, used = {}, [0, 0]
        for w, g, u in BEFORE + [(w, g, unit_of(w, g, row)) for row in range(UNITS + 1) for w, g, _ in ROW]:
            if 0 <= u < UNITS and (w, g, u) not in ordinal:
                ordinal[(w, g, u)] = used[bank_of[(w, g)]]
                used[bank_of[(w, g)]] += 1

        def use(what, g, u):
            b = bank_of[(what, g)]
            if isinstance(u, int):
                return b, ordinal[(what, g, u)]
            some = 4
            return b, u * per_row[b] + (ordinal[(what, g, some)] - some * per_row[b])

        def bank_written(eng, what, g, u):
            b, n = use(what, g, u)
            eng.wait_ge(misc_ps[b], n + 1)
            return psM[b], misc_free[b]

        def open_bank(pe, what, g, u):
            b, n = use(what, g, u)
            if not (isinstance(n, int) and n == 0):
                pe.wait_ge(misc_free[b], n)
            return psM[b], misc_ps[b]

        def emptied(eng, what, g, u):
            b, n = use(what, g, u)
            eng.wait_ge(misc_free[b], n + 1)

        def rows(eng, quarter):
            def row(u, p):
                for g in range(NG):
                    quarter(u, g, p)

            row(0, 0)
            with eng.Fori(0, UNITS // 2 - 2) as i:
                row(2 * i + 1, 1)
                row(2 * i + 2, 0)
            for u in range(UNITS - 3, UNITS):
                row(u, u % 2)

        def there(u):
            return not isinstance(u, int) or 0 <= u < UNITS

        MIDDLE = [(1, 2), (2, 0)]
        SLOTS_IN = 16 * sum(len(runs) for runs in PARTS)
        S_AHEAD = [(2, 0), (3, 0), (0, 1), (1, 1)]

        block = st.enter_context(nc.Block())

        def apart(dve):
            carried.append(len(carried) % 8)
            dve.memset(carry[:, carried[-1]:carried[-1] + 1], 0.0)

        carried = []

        def batches(eng, two):
            two(0, None)
            with eng.Fori(1, B // 2 - 1) as i:
                two(i, i - 1)
            two(B // 2 - 1, B // 2 - 2)
            two(None, B // 2 - 1)

        @block.sync
        def _(sp):
            sp.dma_start(encT[:], ctx_t.rearrange("(k p) n -> p k n", p=P)).then_inc(wa_in, 16)
            sp.dma_start(wa[:], waT.rearrange("(k p) n -> p k n", p=P)).then_inc(wa_in, 16)
            sp.dma_start(acc[:], x.rearrange("b (t p) e -> p (b t) e", p=P)).then_inc(x_in, 16)
            sp.dma_start(pt[:], p_t.partition_broadcast(P)).then_inc(bc_in, 16)
            sp.dma_start(len_i[:], src_len.partition_broadcast(P)).then_inc(bc_in, 16)
            for dst, src in ((wc, wcT.rearrange("(k p) n -> p k n", p=P)),
                             (rw1, rw1T.rearrange("(k p) n -> p k n", p=P)),
                             (rw2, rw2T), (obr, ob), (bqk, qkb),
                             (rb1_b, rb1.partition_broadcast(P)), (lng_b, ln_g.partition_broadcast(P)),
                             (lnb_b, ln_b.partition_broadcast(P)), (rb2_b, rb2.partition_broadcast(P))):
                sp.dma_start(dst[:], src).then_inc(const_in, 16)
            for q in range(2):
                sp.dma_start(enc[q][:], ctx_e[q]).then_inc(enc_in[q], 16)
            with sp.Fori(1, B // 2) as i:
                for q in range(2):
                    sp.wait_ge(cx_ps, 2 * i + (q - 1))
                    sp.dma_start(enc[q][:], ctx_e[2 * i + q]).then_inc(enc_in[q], 16)

            def load_qk(p, jo):
                for n, w in enumerate((qwT, kwT)):
                    sp.dma_start(wqkv[p][:, n], w[2 * jo + p].rearrange("(k p) o -> p k o", p=P)).then_inc(wqk_in[p], 16)

            def load_v(p, jo):
                e = 2 * jo + p
                sp.dma_start(wqkv[p][:, 2], vwT[e].rearrange("(k p) o -> p k o", p=P)).then_inc(wv_in[p], 16)
                sp.dma_start(bv[p][:], vb[e].partition_broadcast(P)).then_inc(wv_in[p], 16)

            def load_o(p, jo):
                sp.dma_start(wo[p][:], owT[2 * jo + p].rearrange("(k p) o -> p k o", p=P)).then_inc(wo_in, 16)

            def load_x(p, b):
                sp.dma_start(xs[p][:], xT[:, b]).then_inc(xs_in[p], 16)

            def send_max(p, g, u):
                emptied(sp, "m", g, u)
                sp.dma_start(Qp[p][KR:KM, G * g:G * g + G, :], mT[g % 2][:]).then_inc(mrow_in, 16)

            def parts_to_dram(n, low, u):
                if low:
                    sp.wait_ge(split_made, 2 * u + n + 1)
                    sp.dma_start(packed[n][1:3].rearrange("m p f -> p m f"),
                                 parts[n][:, 1:3].rearrange("p m k s -> p m (k s)")).then_inc(parts_out, 16)
                else:
                    sp.wait_ge(hi_made, 2 * u + n + 1)
                    sp.dma_start(packed[n][0], parts[n][:, 0].rearrange("p k s -> p (k s)")).then_inc(parts_out, 16)

            def slots_from_dram(n, p, runs):
                for run, at in PARTS[n][runs]:
                    sp.dma_start((Qp, Kp)[n][p][D * at:D * at + D * len(run)].rearrange("p h s -> p (h s)"),
                                 packed[n][run[0]:run[0] + len(run)].rearrange("m (r h) f -> (m r) (h f)", r=D)
                                 ).then_inc(slots_in, 16)

            def before_slots(u):
                sp.wait_ge(parts_out, 64 * u + 64)
                if not (isinstance(u, int) and u < 2):
                    sp.wait_ge(t_ps, H * u - H)

            for p in range(2):
                load_qk(p, 0)
                load_v(p, 0)
                load_o(p, 0)
            sp.wait_ge(wo_in, 32)
            sp.wait_ge(hn2T_made, B)
            load_x(0, 0)
            load_x(1, 0)
            for u in range(2):
                for n in range(2):
                    parts_to_dram(n, False, u)
                for n in range(2):
                    parts_to_dram(n, True, u)
                if u == 0:
                    before_slots(0)
                    for n in (1, 0):
                        slots_from_dram(n, 0, slice(None))
                    sp.wait_ge(slots_in, SLOTS_IN)
            send_max(0, 0, 0)

            def store(b, u):
                emptied(sp, "o", 0, u)
                sp.dma_start(out[b].rearrange("(t p) e -> p t e", p=P),
                             acc[:, bass.ds(TT * b, TT), :]).then_inc(stored, 16)

            def row(jo, b, p):
                u = 2 * b + (2 * B * jo + p)
                first, last = (isinstance(b, int) and b == n for n in (0, B - 1))
                if first and p == 1 and jo > 0:
                    sp.wait_ge(wo_in, 32 * (jo + 1))
                one_more = not (last and p == 1 and jo + 1 == NJ)
                two_more = not (last and jo + 1 == NJ)
                if one_more:
                    before_slots(u + 1)
                    slots_from_dram(1, 1 - p, slice(0, 1))
                send_max(p, 1, u)
                if one_more:
                    slots_from_dram(1, 1 - p, slice(1, None))
                    slots_from_dram(0, 1 - p, slice(None))
                send_max(p, 2, u)
                if two_more:
                    load_x(p, 0 if last else b + 1)
                if last and jo + 1 < NJ:
                    load_v(p, jo + 1)
                if jo + 1 < NJ and (isinstance(b, int) and (b, p) in ((B - 2, 1), (B - 1, 0))):
                    load_qk(1 - p, jo + 1)
                if two_more:
                    sp.wait_ge(slots_in, SLOTS_IN * u + 2 * SLOTS_IN)
                    parts_to_dram(0, False, u + 2)
                    parts_to_dram(0, True, u + 2)
                    parts_to_dram(1, False, u + 2)
                send_max(p, 3, u)
                if two_more:
                    parts_to_dram(1, True, u + 2)
                if one_more:
                    send_max(1 - p, 0, u + 1)
                if last and p == 1 and jo + 1 < NJ:
                    emptied(sp, "o", 0, u - 1)
                    load_o(0, jo + 1)
                if first and p == 0 and jo > 0:
                    emptied(sp, "o", 0, u - 1)
                    load_o(1, jo)

                if jo == NJ - 1 and p == 0 and not first:
                    store(b - 1, u - 1)

            for jo in range(NJ):
                for p in range(2):
                    row(jo, 0, p)
                with sp.Fori(1, B - 2) as b:
                    for p in range(2):
                        row(jo, b, p)
                for b in (B - 2, B - 1):
                    for p in range(2):
                        row(jo, b, p)
            store(B - 1, UNITS - 1)
            sp.wait_ge(stored, 16 * B)
            for p in range(2):
                sp.wait_ge(xs_in[p], 8 * UNITS)
            sp.wait_ge(mrow_in, 16 * NG * UNITS)
            sp.wait_ge(parts_out, 64 * UNITS)
            sp.wait_ge(slots_in, SLOTS_IN * UNITS)

        @block.gpsimd
        def _(pool):
            own = Step(pool, pool_step)
            own.begin(0, 3)
            own(pool.memset(ident[:], 0.0))
            own(pool.affine_select(out=ident[:], in_=ident[:], compare_op=ALU.not_equal, fill=1.0, base=0,
                                   pattern=[[-1, P]], channel_multiplier=1))
            pool.tensor_copy(ident_bf[:], ident[:]).then_inc(ident_made, 1)
            pool.iota(idx[:], pattern=[[1, L]], base=0, channel_multiplier=0,
                      allow_small_or_imprecise_dtypes=True).then_inc(iota_made, 1)
            pool.iota(rank[:], pattern=[[-1, NE]], base=NE, channel_multiplier=0,
                      allow_small_or_imprecise_dtypes=True).then_inc(iota_made, 1)
            for p in range(2):
                pool.memset(vaug[p][:, :, :, D:V1], 1.0)
            own(pool.memset(mhalf[:], -0.5))
            own.end(1)
            own.begin(0, 2)
            for p in range(2):
                own(pool.memset(Kp[p][KR:KM], 1.0))
            own.end(1)
            with pool.Fori(0, 3 * B // 2) as n:
                for q in range(2):
                    pool.wait_ge(var_made, 2 * n + (q + 1))
                    pool.tensor_tensor(rstd[q][:], veps[q][:], mhalf[:], ALU.pow).then_inc(rstd_made, 1)

            def unit(u):
                for n in range(2):
                    pool.wait_ge(hi_made, 2 * u + n + 1)
                    pool.tensor_tensor(rest[n][:], x32[n][:], parts[n][:, 0], ALU.subtract).then_inc(rest_made, 1)
                    pool.wait_ge(mid_made, 2 * u + n + 1)
                    pool.tensor_tensor(parts[n][:, 2], rest[n][:], parts[n][:, 1],
                                       ALU.subtract).then_inc(split_made, 1)

            for u in range(2):
                unit(u)
            with pool.Fori(2, UNITS) as u:
                unit(u)

        @block.tensor
        def _(pe):
            pe.wait_ge(ident_made, 1)
            pe.wait_ge(wa_in, 32)
            half = B * L // 2
            for m in range(KT):
                for c in range(2):
                    for k in range(KT):
                        mm = pe.matmul(psS[0][:, 0:half] if (m, c) == (0, 0) else
                                       [psS[1], psS[2], psT[0]][2 * m + c - 1][:, 0:half],
                                       wa[:, k, m * P:m * P + P], encT[:, k, c * half:c * half + half],
                                       start=(k == 0), stop=(k == KT - 1))
                    mm.then_inc(waenc_ps, 1)
            pe.wait_ge(waenc_made, 4)
            pe.wait_ge(const_in, 16 * 9)

            def turn(hn, bank):
                for k in range(KT):
                    for t in range(TT):
                        mm = pe.transpose(bank[:, k * S + t * P:k * S + t * P + P],
                                          hn[:, t, k * P:k * P + P], ident[:])
                return mm

            def two(i, r):
                for q in range(2):
                    if i is not None:
                        pe.wait_ge(hn1_made, 2 * i + (q + 1))
                        turn(hn1[q], bank_a[q]).then_inc(hn1T_ps, 1)
                for q in range(2):
                    if r is not None:
                        pe.wait_ge(hn2_made, 2 * r + (q + 1))
                        turn(hn2[q], bank_r[q]).then_inc(hn2T_ps, 1)
                for q in range(2):
                    if i is not None:
                        pe.wait_ge(hn1T_made, 2 * i + (q + 1))
                        for t in range(TT):
                            for k in range(KT):
                                mm = pe.matmul(bank_b[q][:, t * L:t * L + L], hn1T[q][:, k, t * P:t * P + P],
                                               waenc[:, k, bass.ds((2 * i + q) * L, L)],
                                               start=(k == 0), stop=(k == KT - 1))
                        mm.then_inc(score_ps, 1)
                for q in range(2):
                    if r is not None:
                        pe.wait_ge(hn2T_made, 2 * r + (q + 1))
                        for t in range(TT):
                            for k in range(KT):
                                mm = pe.matmul(bank_r[q][:, t * R:t * R + R], hn2T[q][:, k, t * P:t * P + P],
                                               rw1[:, k, :], start=(k == 0), stop=(k == KT - 1))
                        mm.then_inc(rh_ps, 1)
                if i is not None:
                    for q in range(2):
                        for t in range(TT):
                            for k in range(KT):
                                pe.matmul(bank_d[q][:, t * E:t * E + E], hn1T[q][:, k, t * P:t * P + P],
                                          wc[:, KT + k, :], start=(t == 0 and k == 0), stop=False)
                    for q in range(2):
                        pe.wait_ge(al_made, 2 * i + (q + 1))
                        for t in range(TT):
                            mm = pe.transpose(bank_b[q][0:L, S + t * P:S + t * P + P], al[q][:, t, :], ident[:])
                        mm.then_inc(alT_ps, 1)
                    for q in range(2):
                        pe.wait_ge(alT_made, 2 * i + (q + 1))
                        pe.wait_ge(enc_in[q], 16 * i + 16)
                        for k in range(KT):
                            mm = pe.matmul(bank_a[q][:, k * S:k * S + S], enc[q][:, k * P:k * P + P], alT[q][:],
                                           start=True, stop=True)
                        mm.then_inc(cx_ps, 1)
                for q in range(2):
                    if r is not None:
                        pe.wait_ge(rh_made, 2 * r + (q + 1))
                        for t in range(TT):
                            mm = pe.transpose(bank_r[q][:, S + t * P:S + t * P + P], rh[q][:, t, :], ident[:])
                        mm.then_inc(rhT_ps, 1)
                for q in range(2):
                    if i is not None:
                        pe.wait_ge(cx_made, 2 * i + (q + 1))
                        for t in range(TT):
                            for k in range(KT):
                                mm = pe.matmul(bank_d[q][:, t * E:t * E + E], cxT[q][:, k, t * P:t * P + P],
                                               wc[:, k, :], start=False, stop=(t == TT - 1 and k == KT - 1))
                        mm.then_inc(co_ps, 1)
                for q in range(2):
                    if r is not None:
                        pe.wait_ge(rhT_made, 2 * r + (q + 1))
                        for t in range(TT):
                            mm = pe.matmul(bank_r[q][:, t * NE:t * NE + NE], rhT[q][:, t * P:t * P + P], rw2[:],
                                           start=True, stop=True)
                        mm.then_inc(lg_ps, 1)

            batches(pe, two)

            def project(what, n, p, u):
                ps, written = open_bank(pe, what, 0, u)
                for m in range(2):
                    for k in range(KT):
                        c = slice(m * P, m * P + P)
                        mm = (pe.matmul(ps[:, m * S:m * S + S], wqkv[p][:, n, k, c], xT[:, u % (2 * B) // 2, k, :],
                                        start=(k == 0), stop=(k == KT - 1)) if n < 2 else
                              pe.matmul(ps[:, m * E:m * E + E], xs[p][:, k, c], wqkv[p][:, n, k, :],
                                        start=(k == 0), stop=(k == KT - 1)))
                mm.then_inc(written, 1)

            def turn_max(g, u):
                pe.wait_ge(mhl_made, 4 * u + g + 1)
                ps, written = open_bank(pe, "m", g, u)
                for t in range(TT):
                    mm = pe.transpose(ps[:].bitcast(BF16)[0:2 * G, t * P:t * P + P], mhl[g % 2][:, t, :], ident_bf[:])
                mm.then_inc(written, 1)

            def scores(p, g, j, u):
                h = G * g + j
                if h == 0:
                    pe.wait_ge(slots_in, SLOTS_IN * u + SLOTS_IN)
                n = H * u + h
                if not (isinstance(n, int) and n < BACK[j]):
                    pe.wait_ge(max_made, n - BACK[j] + 1)
                for t in range(TT):
                    mm = pe.matmul(psS[S_BANK[j]][:, t * S:t * S + S], Qp[p][0:KR, h, t * P:t * P + P],
                                   Kp[p][0:KR, h, :], start=True, stop=True)
                mm.then_inc(s_ps, 1)

            def scores_T(p, h, u):
                n = H * u + h
                if not (isinstance(n, int) and n < 2):
                    pe.wait_ge(exp_made, n - 1)
                for k in range(TT):
                    mm = pe.matmul(psT[h % 2][:, k * S:k * S + S], Kp[p][0:KM, h, k * P:k * P + P],
                                   Qp[p][0:KM, h, :], start=True, stop=True)
                mm.then_inc(t_ps, 1)

            def values(p, h, u):
                g, j = h // G, h % G
                if h == 0:
                    emptied(pe, "v", 0, u)
                if j == 0 and not (isinstance(u, int) and NG * u + g == 0):
                    pe.wait_ge(oun_made, NG * u + g)
                pe.wait_ge(exp_made, H * u + h + 1)
                for k in range(TT):
                    mm = pe.matmul(psV[32 * j:32 * j + V1, (g % 2) * S:(g % 2) * S + S],
                                   vaug[p][:, k, h, :], pexp[h % NP_][:, k, :],
                                   start=(k == 0), stop=(k == TT - 1))
                if j == G - 1:
                    mm.then_inc(pv_ps, 1)

            def by_token(p, t, u):
                pe.wait_ge(oun_made, NG * u + NG)
                ps, written = open_bank(pe, "t1", t, u)
                for g in range(NG):
                    mm = pe.transpose(ps[:, g * P:g * P + P], oun[p][:, g, t * P:t * P + P], ident[:])
                mm.then_inc(written, 1)

            def by_width(u):
                for t in range(TT):
                    emptied(pe, "t1", t, u)
                ps, written = open_bank(pe, "t2", 0, u)
                for k in range(KT):
                    for t in range(TT):
                        mm = pe.transpose(ps[:, k * S + t * P:k * S + t * P + P],
                                          onm[:, t, k * H // KT:(k + 1) * H // KT, :].rearrange("p h d -> p (h d)"),
                                          ident[:])
                mm.then_inc(written, 1)

            def output(p, u):
                emptied(pe, "t2", 0, u)
                ps, written = open_bank(pe, "o", 0, u)
                for t in range(TT):
                    for k in range(KT):
                        mm = pe.matmul(ps[:, t * E:t * E + E], onT[:, k, t * P:t * P + P], wo[p][:, k, :],
                                       start=(k == 0), stop=(k == KT - 1))
                mm.then_inc(written, 1)

            def extra(what, g, p, u):
                if what == "m":
                    turn_max(g, u)
                elif what == "t1":
                    by_token(p, g, u)
                elif what == "t2":
                    by_width(u)
                elif what == "o":
                    output(p, u)
                else:
                    if what == "pq":
                        pe.wait_ge(wqk_in[p], 32 * (u // (2 * B)) + 32)
                    elif what == "v":
                        pe.wait_ge(wv_in[p], 32 * (u // (2 * B)) + 32)
                        pe.wait_ge(xs_in[p], 8 * (u - p) + 16)
                    project(what, {"pq": 0, "pk": 1, "v": 2}[what], p, u)

            extra("pq", 0, 0, 0)
            extra("pk", 0, 0, 0)
            extra("v", 0, 0, 0)
            extra("pq", 0, 1, 1)
            extra("pk", 0, 1, 1)
            pe.wait_ge(gt_made, 1)
            banks = [psS[0], psS[1], psS[2], psT[0]]
            for t in range(NT):
                mm = pe.transpose(banks[t // 4][0:NE, (t % 4) * P:(t % 4) * P + P], gt[:, t, :], ident[:])
            mm.then_inc(gT_ps, 1)
            pe.wait_ge(gT_made, 1)
            for b in range(B):
                if b > 1:
                    pe.wait_ge(ob_added, b - 1)
                for t in range(TT):
                    mm = pe.matmul(bank_ob[b % 2][:, t * E:t * E + E], gT[:, TT * b + t, :], obr[:],
                                   start=True, stop=True)
                mm.then_inc(ob_ps, 1)
            pe.wait_ge(ob_added, B)
            for j in range(G):
                scores(0, 0, j, 0)
            turn_max(0, 0)
            for j in range(G):
                scores(0, 1, j, 0)

            def quarter(u, g, p):
                sg, du = S_AHEAD[g]
                pe.wait_ge(mrow_in, 16 * NG * u + 16 * (g + 1))
                for j in range(G):
                    if there(u + du):
                        scores((p + du) % 2, sg, j, u + du)
                    h = G * g + j
                    scores_T(p, h, u)
                    if j != 2:
                        if h >= 2:
                            values(p, h - 2, u)
                        elif there(u - 1):
                            values(1 - p, H + h - 2, u - 1)
                    for what, eg, _ in EXTRAS[g][j]:
                        v = unit_of(what, eg, u)
                        if there(v):
                            extra(what, eg, (p + unit_of(what, eg, 0)) % 2, v)
                    if j == 2:
                        values(p, h - 2, u)

            rows(pe, quarter)
            values(1, H - 2, UNITS - 1)
            values(1, H - 1, UNITS - 1)
            for what, eg in (("t1", 0), ("t1", 1), ("t2", 0), ("o", 0)):
                extra(what, eg, 1, UNITS - 1)

        @block.scalar
        def _(act):
            act.wait_ge(gauss_arg, 1)
            act.activation(gauss[:], gauss[:], ACT.Exp, scale=-1.0 / DEV_POW).then_inc(gauss_made, 1)
            half = B * L // 2
            for n in range(4):
                act.wait_ge(waenc_ps, n + 1)
                src = [psS[0], psS[1], psS[2], psT[0]][n]
                act.activation(waenc[:, n // 2, (n % 2) * half:(n % 2) * half + half], src[:, 0:half],
                               ACT.Copy).then_inc(waenc_made, 1)
            def flat(a):
                return a[:].rearrange("p k s -> p (k s)")

            def two(i, r):
                for q in range(2):
                    if i is not None:
                        act.wait_ge(hn1T_ps, 2 * i + (q + 1))
                        act.activation(flat(hn1T[q]), bank_a[q][:], ACT.Copy).then_inc(hn1T_made, 1)
                for q in range(2):
                    if r is not None:
                        act.wait_ge(hn2T_ps, 2 * r + (q + 1))
                        act.activation(xT[:, 2 * r + q].rearrange("p k s -> p (k s)"), bank_r[q][:], ACT.Copy)
                        act.activation(flat(hn2T[q]), bank_r[q][:], ACT.Copy).then_inc(hn2T_made, 1)
                if i is not None:
                    for q in range(2):
                        act.wait_ge(smax_made, 2 * i + (q + 1))
                        for t in range(TT):
                            act.activation(sc[q][:, t, :], sc[q][:, t, :], ACT.Exp, bias=smx[q][:, t:t + 1],
                                           accum_out=ssum[q][:, t:t + 1]).then_inc(sexp_made, 1)
                    for q in range(2):
                        act.wait_ge(alT_ps, 2 * i + (q + 1))
                        act.activation(alT[q][:], bank_b[q][0:L, S:2 * S], ACT.Copy).then_inc(alT_made, 1)
                    for q in range(2):
                        act.wait_ge(cx_ps, 2 * i + (q + 1))
                        act.activation(flat(cxT[q]), bank_a[q][:], ACT.Copy).then_inc(cx_made, 1)
                for q in range(2):
                    if r is not None:
                        act.wait_ge(rhT_ps, 2 * r + (q + 1))
                        act.activation(rhT[q][:], bank_r[q][:, S:2 * S], ACT.Copy).then_inc(rhT_made, 1)
                for q in range(2):
                    if i is not None:
                        act.wait_ge(co_ps, 2 * i + (q + 1))
                        act.activation(flat(th[q]), bank_d[q][:], ACT.Tanh).then_inc(tanh_made, 1)

            batches(act, two)

            def keep_max(g, u):
                ps, free = bank_written(act, "m", g, u)
                act.activation(mT[g % 2][:], ps[:].bitcast(BF16)[0:2 * G, 0:S], ACT.Copy).then_inc(free, 1)

            def middle(n, u):
                act.wait_ge(rest_made, 2 * u + n + 1)
                act.activation(parts[n][:, 1], rest[n][:], ACT.Copy).then_inc(mid_made, 1)

            middle(0, 0)
            middle(1, 0)
            act.wait_ge(lsub_made, 1)
            act.activation(pr[:], lg[:], ACT.Exp).then_inc(lexp_made, 1)
            act.wait_ge(gT_ps, 1)
            for n in range(4):
                last = act.activation(gT[:, 4 * n:4 * n + 4, :].rearrange("p a b -> p (a b)"),
                                      [psS[0], psS[1], psS[2], psT[0]][n][0:NE, :], ACT.Copy)
            last.then_inc(gT_made, 1)
            middle(0, 1)
            middle(1, 1)
            keep_max(0, 0)

            def undivided(p, g, u):
                act.wait_ge(pv_ps, NG * u + g + 1)
                act.activation(oun[p][:, g, :], psV[:, (g % 2) * S:(g % 2) * S + S], ACT.Copy).then_inc(oun_made, 1)

            def keep_on(u):
                ps, free = bank_written(act, "t2", 0, u)
                act.activation(onT[:].rearrange("p k s -> p (k s)"), ps[:], ACT.Copy).then_inc(free, 1)

            def quarter(u, g, p):
                for j in range(G):
                    h = G * g + j
                    act.wait_ge(t_ps, H * u + h + 1)
                    act.activation(pexp[h % NP_][:].rearrange("p k s -> p (k s)"), psT[h % 2][:],
                                   ACT.Exp, scale=SCALE).then_inc(exp_made, 1)
                    if j == 1:
                        if g > 0:
                            undivided(p, g - 1, u)
                        elif there(u - 1):
                            undivided(1 - p, NG - 1, u - 1)
                    if there(u + 2) and (g, j) in MIDDLE:
                        middle(MIDDLE.index((g, j)), u + 2)
                    for what, eg, _ in EXTRAS[g][j]:
                        v = unit_of(what, eg, u)
                        if there(v):
                            if what == "m":
                                keep_max(eg, v)
                            elif what == "t2":
                                keep_on(v)

            rows(act, quarter)
            undivided(1, NG - 1, UNITS - 1)
            keep_on(UNITS - 1)

        @block.vector
        def _(dve):
            own = Step(dve, dve_step)
            own.begin(0, 8)
            dve.memset(psV[:], 0.0)
            dve.wait_ge(iota_made, 2)
            dve.wait_ge(bc_in, 32)
            own(dve.tensor_scalar(w_start[:], pt[:], -WINDOW, 0.0, ALU.add, ALU.max))
            own(dve.tensor_scalar(w_end[:], pt[:], WINDOW, None, ALU.add))
            own(dve.tensor_copy(len_f[:], len_i[:]))
            own(dve.tensor_tensor(w_end[:], w_end[:], len_f[:], ALU.min))
            idx_b = idx[:].unsqueeze(1).to_broadcast([P, B, L])

            def per_batch(a):
                return a[:].unsqueeze(2).to_broadcast([P, B, L])

            own(dve.tensor_tensor(keep[:], idx_b, per_batch(w_start), ALU.is_ge))
            own(dve.tensor_tensor(keep2[:], idx_b, per_batch(w_end), ALU.is_le))
            own(dve.tensor_tensor(keep[:], keep[:], keep2[:], ALU.mult))
            dve.tensor_scalar(fill[:], keep[:], NEG, -NEG, ALU.mult, ALU.add)
            own(dve.tensor_tensor(gauss[:], idx_b, per_batch(pt), ALU.subtract))
            dve.tensor_tensor(gauss[:], gauss[:], gauss[:], ALU.mult).then_inc(gauss_arg, 1)
            own.end(1)
            dve.wait_ge(gauss_made, 1)
            dve.wait_ge(x_in, 16)
            dve.wait_ge(const_in, 16 * 9)

            def stats_of(tiles, q):
                for t in range(TT):
                    last = dve.bn_stats(stats[q][:, t, :], tiles[t])
                own(last, apart)
                for t in range(TT):
                    last = dve.bn_aggr(mv[q][:, t, :], stats[q][:, t, :])
                own(last)
                dve.tensor_scalar(veps[q][:], mv[q][:, :, 1], EPS, None, ALU.add).then_inc(var_made, 1)

            def normalise(dst, tiles, n, q):
                dve.wait_ge(rstd_made, n + 1)
                for t in range(TT):
                    last = dve.tensor_scalar(dst[:, t, :], tiles[t], mv[q][:, t, 0:1], rstd[q][:, t:t + 1],
                                             ALU.subtract, ALU.mult)
                return last

            def norm_1(i):
                tiles = [[acc[:, TT * (2 * i + q) + t, :] for t in range(TT)] for q in range(2)]
                for q in range(2):
                    stats_of(tiles[q], q)
                for q in range(2):
                    before = q if isinstance(i, int) and i == 0 else 6 * i + (q - 4)
                    normalise(hn1[q], tiles[q], before, q).then_inc(hn1_made, 1)

            def two(i, r):
                last = isinstance(i, int) and i == B // 2 - 1
                per = (0 if i is None else 14 if last else 18) + (0 if r is None else 14)
                looped = i is not None and not isinstance(i, int)
                own.begin(r if looped else 0, per)
                if i is not None:
                    for q in range(2):
                        dve.wait_ge(score_ps, 2 * i + (q + 1))
                        kb_ = keep[:, bass.ds(2 * i + q, 1), :].to_broadcast([P, TT, L])
                        fb_ = fill[:, bass.ds(2 * i + q, 1), :].to_broadcast([P, TT, L])
                        own(dve.tensor_tensor(sc[q][:], bank_b[q][:, 0:TT * L].rearrange("p (t l) -> p t l", t=TT),
                                              kb_, ALU.mult))
                        own(dve.tensor_tensor(sc[q][:], sc[q][:], fb_, ALU.add))
                        dve.tensor_reduce(smx[q][:], sc[q][:], AX.X, ALU.max, negate=True).then_inc(smax_made, 1)
                rtiles = [[rh[q][:, t, :] for t in range(TT)] for q in range(2)]
                if r is not None:
                    for q in range(2):
                        dve.wait_ge(rh_ps, 2 * r + (q + 1))
                        own(dve.tensor_tensor(rh[q][:], bank_r[q][:, 0:TT * R].rearrange("p (t r) -> p t r", t=TT),
                                              rb1_b[:].unsqueeze(1).to_broadcast([P, TT, R]), ALU.add))
                        stats_of(rtiles[q], q)
                if i is not None:
                    for q in range(2):
                        dve.wait_ge(sexp_made, 4 * i + (TT * q + TT))
                        own(dve.reciprocal(ssum[q][:], ssum[q][:]))
                        own(dve.tensor_tensor(sc[q][:], sc[q][:], ssum[q][:].unsqueeze(2).to_broadcast([P, TT, L]),
                                              ALU.mult))
                        dve.tensor_tensor(al[q][:], sc[q][:],
                                          gauss[:, bass.ds(2 * i + q, 1), :].to_broadcast([P, TT, L]),
                                          ALU.mult).then_inc(al_made, 1)
                if r is not None:
                    for q in range(2):
                        before = 6 * r + 6 - (2 if i is None else 0)
                        own(normalise(rh[q], rtiles[q], before + q, q))
                        own(dve.tensor_tensor(rh[q][:], rh[q][:], lng_b[:].unsqueeze(1).to_broadcast([P, TT, R]),
                                              ALU.mult))
                        own(dve.tensor_tensor(rh[q][:], rh[q][:], lnb_b[:].unsqueeze(1).to_broadcast([P, TT, R]),
                                              ALU.add))
                        dve.tensor_scalar(rh[q][:], rh[q][:], 0.0, None, ALU.max).then_inc(rh_made, 1)
                if i is not None:
                    if not last:
                        norm_1(i + 1)
                    for q in range(2):
                        tiles = [acc[:, TT * (2 * i + q) + t, :] for t in range(TT)]
                        pair = acc[:, bass.ds(TT * (2 * i + q), TT), :]
                        dve.wait_ge(tanh_made, 2 * i + (q + 1))
                        own(dve.tensor_tensor(pair, pair, th[q][:], ALU.add), apart)
                        stats_of(tiles, q)
                if r is not None:
                    for q in range(2):
                        dve.wait_ge(lg_ps, 2 * r + (q + 1))
                        own(dve.tensor_tensor(lg[:, bass.ds(TT * (2 * r + q), TT), :],
                                              bank_r[q][:, 0:TT * NE].rearrange("p (t e) -> p t e", t=TT),
                                              rb2_b[:].unsqueeze(1).to_broadcast([P, TT, NE]), ALU.add))
                if i is not None:
                    for q in range(2):
                        tiles = [acc[:, TT * (2 * i + q) + t, :] for t in range(TT)]
                        normalise(hn2[q], tiles, 6 * i + (2 if last else 4) + q, q).then_inc(hn2_made, 1)
                own.end(B // 2 - 2 if looped else 1)

            own.begin(0, 4)
            norm_1(0)
            own.end(1)
            batches(dve, two)

            def keep_32(what, n, u):
                ps, free = bank_written(dve, what, 0, u)
                if not (isinstance(u, int) and u == 0):
                    dve.wait_ge(split_made, 2 * u)
                    dve.wait_ge(parts_out, 64 * u)
                e = 2 * (u // (2 * B)) + u % 2
                dve.tensor_tensor(x32[n][:], ps[:].rearrange("p (k s) -> p k s", k=KT),
                                  bqk[:, bass.ds(NE * n + e, 1), :].rearrange("p o k -> p k o")
                                  .to_broadcast([P, KT, S]), ALU.add).then_inc(free, 1)
                emptied(dve, what, 0, u)
                dve.tensor_copy(parts[n][:, 0], x32[n][:]).then_inc(hi_made, 1)

            def keep_v(p, u):
                ps, free = bank_written(dve, "v", 0, u)
                dve.tensor_tensor(vaug[p][:, :, :, 0:D], ps[:].rearrange("p (t h d) -> p t h d", t=TT, h=H),
                                  bv[p][:].rearrange("p (h d) -> p h d", h=H).unsqueeze(1)
                                  .to_broadcast([P, TT, H, D]), ALU.add).then_inc(free, 1)

            def head_max(g, j, u):
                dve.wait_ge(s_ps, 16 * u + G * g + j + 1)
                dve.tensor_reduce(negm[g % 2][:, :, j], psS[S_BANK[j]][:].rearrange("p (t s) -> p t s", t=TT), AX.X,
                                  ALU.max, negate=True).then_inc(max_made, 1)

            def split_max(g, u):
                dve.wait_ge(max_made, 16 * u + G * g + G)
                dve.tensor_copy(mhl[g % 2][:, :, 0:G], negm[g % 2][:]).then_inc(mhi_made, 1)
                dve.wait_ge(mhi_made, 4 * u + g + 1)
                dve.tensor_tensor(mhl[g % 2][:, :, G:2 * G], negm[g % 2][:], mhl[g % 2][:, :, 0:G],
                                  ALU.subtract).then_inc(mhl_made, 1)

            keep_32("pq", 0, 0)
            keep_32("pk", 1, 0)
            keep_v(0, 0)

            def per_token(a):
                return a[:].unsqueeze(2).to_broadcast([P, NT, NE])

            rank_b = rank[:].unsqueeze(1).to_broadcast([P, NT, NE])
            own.begin(0, 18)
            own(dve.tensor_reduce(r1[:], lg[:], AX.X, ALU.max))
            dve.tensor_tensor(lg[:], lg[:], per_token(r1), ALU.subtract).then_inc(lsub_made, 1)
            dve.wait_ge(lexp_made, 1)
            own(dve.reduce_sum(r2[:], pr[:], AX.X))
            own(dve.reciprocal(r2[:], r2[:]))
            own(dve.tensor_tensor(pr[:], pr[:], per_token(r2), ALU.mult))

            def pick(src, top, one_hot):
                own(dve.tensor_reduce(top[:], src[:], AX.X, ALU.max))
                own(dve.tensor_tensor(eq[:], src[:], per_token(top), ALU.is_equal))
                own(dve.tensor_tensor(eq[:], eq[:], rank_b, ALU.mult))
                own(dve.tensor_reduce(r3[:], eq[:], AX.X, ALU.max))
                own(dve.tensor_tensor(one_hot[:], eq[:], per_token(r3), ALU.is_equal))

            pick(pr, r1, oh1)
            own(dve.scalar_tensor_tensor(pr2[:].rearrange("p a b -> p (a b)"), oh1[:].rearrange("p a b -> p (a b)"),
                                         -2.0, pr[:].rearrange("p a b -> p (a b)"), ALU.mult, ALU.add))
            pick(pr2, r2, oh2)
            own(dve.tensor_tensor(r1[:], r1[:], r2[:], ALU.add))
            own(dve.reciprocal(r1[:], r1[:]))
            own(dve.tensor_tensor(oh1[:], oh1[:], oh2[:], ALU.add))
            own.end(1)
            own.begin(0, 2)
            own(dve.tensor_tensor(oh1[:], oh1[:], pr[:], ALU.mult))
            dve.tensor_tensor(gt[:], oh1[:], per_token(r1), ALU.mult).then_inc(gt_made, 1)
            dve.wait_ge(gt_made, 1)
            for q in range(2):
                last = dve.tensor_copy(
                    gates[:].rearrange("p (j b q t) -> p q j b t", j=NJ, b=B, q=2)[:, q],
                    gt[:].rearrange("p (b t) (j q) -> p q j b t", b=B, j=NJ)[:, q])
            own(last)
            own.end(1)
            keep_32("pq", 0, 1)
            keep_32("pk", 1, 1)
            for b in range(B):
                dve.wait_ge(ob_ps, b + 1)
                a = acc[:, TT * b:TT * b + TT, :]
                dve.tensor_tensor(a, a, bank_ob[b % 2][:].rearrange("p (t e) -> p t e", t=TT),
                                  ALU.add).then_inc(ob_added, 1)
            for g in range(2):
                for j in range(G):
                    head_max(g, j, 0)
                split_max(g, 0)

            def divide(t, u):
                ps, free = bank_written(dve, "t1", t, u)
                heads = ps[:].rearrange("p (h c) -> p h c", h=H)
                dve.reciprocal(rcp[:, t, :], heads[:, :, D]).then_inc(rcp_made, 1)
                dve.wait_ge(rcp_made, 2 * u + t + 1)
                dve.scalar_tensor_tensor(onm[:, t], heads[:, :, 0:D], gates[:, bass.ds(TT * u + t, 1)],
                                         rcp[:, t, :].unsqueeze(2).to_broadcast([P, H, D]), ALU.mult,
                                         ALU.mult).then_inc(free, 1)

            def accumulate(b, u):
                ps, free = bank_written(dve, "o", 0, u)
                a = acc[:, bass.ds(TT * b, TT), :]
                dve.tensor_tensor(a, a, ps[:].rearrange("p (t e) -> p t e", t=TT), ALU.add).then_inc(free, 1)

            def quarter(u, g, p):
                sg, du = S_AHEAD[g]
                for j in range(G):
                    if there(u + du):
                        head_max(sg, j, u + du)
                    if j == G - 1 and there(u + du):
                        split_max(sg, u + du)
                    for what, eg, _ in EXTRAS[g][j]:
                        v = unit_of(what, eg, u)
                        if there(v):
                            vp = (p + unit_of(what, eg, 0)) % 2
                            if what == "t1":
                                divide(eg, v)
                            elif what == "o":
                                accumulate((v - vp) % (2 * B) // 2, v)
                            elif what == "v":
                                keep_v(vp, v)
                            elif what == "pq":
                                keep_32("pq", 0, v)
                            elif what == "pk":
                                keep_32("pk", 1, v)

            rows(dve, quarter)
            divide(0, UNITS - 1)
            divide(1, UNITS - 1)
            accumulate(B - 1, UNITS - 1)


def kernel(**inputs):
    import numpy as np
    import concourse.bacc as bacc
    from concourse.bass_utils import run_bass_kernel_spmd

    def turned(a):
        return np.ascontiguousarray(np.swapaxes(a, -1, -2))

    def by_row(w):
        n, e_out, e_in = w.shape
        return np.ascontiguousarray(w.reshape(n, hp, kt, d, e_in).transpose(0, 4, 2, 3, 1).reshape(n, e_in, e_out))

    heads, kt = 16, 2
    i = {k: np.asarray(v) for k, v in inputs.items()}
    f = {n: i["L0_ffn_" + n] for n in ("rW1", "rb1", "ln_g", "ln_b", "rW2", "rb2", "qW", "qb", "kW", "kb",
                                       "vW", "vb", "oW", "ob")}
    ctx = i["ctx_1024"]
    d = f["qW"].shape[1] // heads
    hp = heads // kt
    arrays = {
        "x": i["x"], "ctx_e": ctx,
        "ctx_t": np.ascontiguousarray(ctx.transpose(2, 0, 1).reshape(ctx.shape[2], -1)),
        "p_t": i["condB_pt"], "src_len": i["_lenS2"],
        "waT": turned(i["L0_xcond_W_a"]), "wcT": turned(i["L0_xcond_W_c"]),
        "rw1T": turned(f["rW1"]), "rb1": f["rb1"], "ln_g": f["ln_g"], "ln_b": f["ln_b"],
        "rw2T": turned(f["rW2"]), "rb2": f["rb2"],
        "qwT": by_row(f["qW"]), "kwT": by_row(f["kW"]),
        "qkb": np.ascontiguousarray(np.stack([f["qb"], f["kb"]]).reshape(-1, hp, kt, d)
                                    .transpose(3, 1, 0, 2).reshape(128, -1, kt)),
        "vwT": turned(f["vW"]), "vb": f["vb"], "owT": turned(f["oW"]), "ob": f["ob"],
    }
    nc = bacc.Bacc("TRN2", target_bir_lowering=False, num_devices=1)
    args = {n: nc.dram_tensor("in_" + n, a.shape, mybir.dt.from_np(a.dtype), kind="ExternalInput").ap()
            for n, a in arrays.items()}
    out = nc.dram_tensor("out_0", i["x"].shape, F32, kind="ExternalOutput").ap()
    pixart_block(nc, out=out, **args)
    r = run_bass_kernel_spmd(nc, [{"in_" + n: np.ascontiguousarray(a) for n, a in arrays.items()}], core_ids=[0])
    return r.results[0]["out_0"]
```
